# Optimizing a Trainium2 kernel written in Bass

```python
import numpy as np
import jax
import jax.numpy as jnp

def _softmax(x, axis=-1):
    return jax.nn.softmax(x, axis=axis)

def _gelu(x):
    return jax.nn.gelu(x, approximate=True)

def _silu(x):
    return jax.nn.silu(x)

def _sigmoid(x):
    return jax.nn.sigmoid(x)

def _layernorm(x, axis=-1, eps=1e-05):
    m = jnp.mean(x, axis=axis, keepdims=True)
    v = jnp.var(x, axis=axis, keepdims=True)
    return (x - m) / jnp.sqrt(v + eps)

def _scatter_add(tgt, idx, src, axis=0):
    return tgt.at[idx].add(src)

def _segment_sum(src, seg, n):
    return jax.ops.segment_sum(src, seg, n)
kernel_name = 'mk_seq_preln_d1_jaxref_r8_d4477a'

def setup_inputs(seed: int=0):
    np.random.seed(seed)
    _w = jnp.asarray

    def _L0_attn_setup():
        import jax, jax.numpy as jnp
        import numpy as np
        HIDDEN = 256
        NUM_HEADS = 16
        NUM_KV_HEADS = 4
        HEAD_DIM = 128
        EPS = 1e-06
        B, S = (2, 256)

        def rms_norm(x, weight, eps=EPS):
            var = jnp.mean(jnp.square(x.astype(jnp.float32)), axis=-1, keepdims=True)
            xn = x.astype(jnp.float32) * jax.lax.rsqrt(var + eps)
            return weight * xn
        key = jax.random.key(seed)
        ks = jax.random.split(key, 5)
        sc_in = 1.0 / np.sqrt(HIDDEN)
        sc_o = 1.0 / np.sqrt(NUM_HEADS * HEAD_DIM)
        x = jax.random.normal(ks[0], (B, S, HIDDEN), dtype=jnp.float32)
        Wq = jax.random.normal(ks[1], (HIDDEN, NUM_HEADS * HEAD_DIM), dtype=jnp.float32) * sc_in
        Wk = jax.random.normal(ks[2], (HIDDEN, NUM_KV_HEADS * HEAD_DIM), dtype=jnp.float32) * sc_in
        Wv = jax.random.normal(ks[3], (HIDDEN, NUM_KV_HEADS * HEAD_DIM), dtype=jnp.float32) * sc_in
        Wo = jax.random.normal(ks[4], (NUM_HEADS * HEAD_DIM, HIDDEN), dtype=jnp.float32) * sc_o
        gq = jnp.ones((HEAD_DIM,), dtype=jnp.float32)
        gk = jnp.ones((HEAD_DIM,), dtype=jnp.float32)
        return {'x': x, 'Wq': Wq, 'Wk': Wk, 'Wv': Wv, 'Wo': Wo, 'gq': gq, 'gk': gk}
    _L0_attn_in = _L0_attn_setup()

    def _L0_ffn_setup():
        import jax, jax.numpy as jnp
        import numpy as np
        HIDDEN = 256
        INTER = 704
        B, S = (2, 256)

        def _ternary(key, shape):
            return jax.random.randint(key, shape, -1, 2).astype(jnp.float32)
        key = jax.random.key(seed)
        ks = jax.random.split(key, 7)
        x = jax.random.normal(ks[0], (B, S, HIDDEN), dtype=jnp.float32)
        gate_w = _ternary(ks[1], (INTER, HIDDEN))
        up_w = _ternary(ks[2], (INTER, HIDDEN))
        down_w = _ternary(ks[3], (HIDDEN, INTER))
        gate_s = jax.random.uniform(ks[4], (INTER,), minval=0.01, maxval=0.1, dtype=jnp.float32)
        up_s = jax.random.uniform(ks[5], (INTER,), minval=0.01, maxval=0.1, dtype=jnp.float32)
        down_s = jax.random.uniform(ks[6], (HIDDEN,), minval=0.01, maxval=0.1, dtype=jnp.float32)
        return {'x': x, 'gate_w': gate_w, 'up_w': up_w, 'down_w': down_w, 'gate_s': gate_s, 'up_s': up_s, 'down_s': down_s}
    _L0_ffn_in = _L0_ffn_setup()
    _d = {'L0_attn_x': _L0_attn_in['x'], 'L0_attn_Wq': _L0_attn_in['Wq'], 'L0_attn_Wk': _L0_attn_in['Wk'], 'L0_attn_Wv': _L0_attn_in['Wv'], 'L0_attn_Wo': _L0_attn_in['Wo'], 'L0_attn_gq': _L0_attn_in['gq'], 'L0_attn_gk': _L0_attn_in['gk'], 'L0_ffn_gate_w': _L0_ffn_in['gate_w'], 'L0_ffn_up_w': _L0_ffn_in['up_w'], 'L0_ffn_down_w': _L0_ffn_in['down_w'], 'L0_ffn_gate_s': _L0_ffn_in['gate_s'], 'L0_ffn_up_s': _L0_ffn_in['up_s'], 'L0_ffn_down_s': _L0_ffn_in['down_s']}
    _x0 = _d['L0_attn_x']
    _d['L0_attn_x'] = jax.random.normal(jax.random.fold_in(jax.random.key(seed), 1), (1, 2048, 256), dtype=_x0.dtype)
    del _x0
    return _d

def reference(L0_attn_x, L0_attn_Wq, L0_attn_Wk, L0_attn_Wv, L0_attn_Wo, L0_attn_gq, L0_attn_gk, L0_ffn_gate_w, L0_ffn_up_w, L0_ffn_down_w, L0_ffn_gate_s, L0_ffn_up_s, L0_ffn_down_s):

    def _L0_attn_ref(x, Wq, Wk, Wv, Wo, gq, gk):
        import jax, jax.numpy as jnp
        import numpy as np
        HIDDEN = 256
        NUM_HEADS = 16
        NUM_KV_HEADS = 4
        HEAD_DIM = 128
        EPS = 1e-06
        B, S = (2, 256)

        def rms_norm(x, weight, eps=EPS):
            var = jnp.mean(jnp.square(x.astype(jnp.float32)), axis=-1, keepdims=True)
            xn = x.astype(jnp.float32) * jax.lax.rsqrt(var + eps)
            return weight * xn
        Bx, Sx, _ = x.shape
        H, KV, D = (NUM_HEADS, NUM_KV_HEADS, HEAD_DIM)
        q = rms_norm((x @ Wq).reshape(Bx, Sx, H, D), gq)
        k = rms_norm((x @ Wk).reshape(Bx, Sx, KV, D), gk)
        v = (x @ Wv).reshape(Bx, Sx, KV, D)
        n_rep = H // KV
        k = jnp.repeat(k, n_rep, axis=2)
        v = jnp.repeat(v, n_rep, axis=2)
        scale = D ** (-0.5)
        attn = jnp.einsum('bqhd,bkhd->bhqk', q, k) * scale
        causal = jnp.tril(jnp.ones((Sx, Sx), dtype=bool))
        attn = jnp.where(causal, attn, -jnp.inf)
        attn = jax.nn.softmax(attn, axis=-1)
        out = jnp.einsum('bhqk,bkhd->bqhd', attn, v).reshape(Bx, Sx, H * D)
        return out @ Wo

    def _L0_ffn_ref(x, gate_w, up_w, down_w, gate_s, up_s, down_s):
        import jax, jax.numpy as jnp
        import numpy as np
        HIDDEN = 256
        INTER = 704
        B, S = (2, 256)

        def _ternary(key, shape):
            return jax.random.randint(key, shape, -1, 2).astype(jnp.float32)
        b, s, h = x.shape
        xf = x.reshape(b * s, h)
        g = jnp.einsum('th,ih->ti', xf, gate_w) * gate_s
        u = jnp.einsum('th,ih->ti', xf, up_w) * up_s
        hdn = jax.nn.silu(g) * u
        out = jnp.einsum('ti,hi->th', hdn, down_w) * down_s
        return out.reshape(b, s, -1)
    x = L0_attn_x
    x = x + _L0_attn_ref(_layernorm(x, axis=-1), L0_attn_Wq, L0_attn_Wk, L0_attn_Wv, L0_attn_Wo, L0_attn_gq, L0_attn_gk)
    x = x + _L0_ffn_ref(_layernorm(x, axis=-1), L0_ffn_gate_w, L0_ffn_up_w, L0_ffn_down_w, L0_ffn_gate_s, L0_ffn_up_s, L0_ffn_down_s)
    return x

_drawn_inputs = setup_inputs


def setup_inputs(seed=0):
    import zlib

    import numpy as np

    out = dict(_drawn_inputs(seed))
    spreads = {'L0_attn_gq': (1.0, 0.6), 'L0_attn_gk': (1.0, 0.6)}
    factors = {}
    for name, (base, spread) in spreads.items():
        noise = np.random.default_rng([zlib.crc32(name.encode()), seed]).standard_normal(out[name].shape)
        drawn = base * np.exp(spread * noise) if base else spread * noise
        out[name] = jnp.asarray(drawn.astype(out[name].dtype))
    for name, factor in factors.items():
        out[name] = (out[name] * factor).astype(out[name].dtype)
    return out
```

```python
from contextlib import ExitStack

import concourse.bass as bass
from concourse import mybir

fp32 = mybir.dt.float32
fp32r = mybir.dt.float32r
bf16 = mybir.dt.bfloat16
ALU = mybir.AluOpType
ACT = mybir.ActivationFunctionType
AX = mybir.AxisListType

P = 128
ROWS = 2048
HID = 256
HEADS = 16
GROUPS = 4
GH = HEADS // GROUPS
D = 128
INTER = 704
BANK = 512
RMS_EPS = 1e-6
LN_EPS = 1e-5
MASKED = -1e30

NT = ROWS // P
CT = HID // P
QW = GH * D
MT = -(-INTER // P)
IPAD = MT * P
CHUNK = BANK
NCH = ROWS // CHUNK
TPC = CHUNK // P
PAIRS = NT // 2
LAG = 2
TBANKS = 3
PBUFS = 4
WQ0, WKV0, WO0 = 0, CT * QW, CT * QW + CT * 2 * D
WCOLS = WO0 + GH * HID


def score_blocks(i):
    n = (i + 1) * P
    return [(b, min(BANK, n - b)) for b in range(0, n, BANK)]


def quarter(n, h):
    return range(n * h // GH, n * (h + 1) // GH)


def group_steps():
    steps = []
    for c in range(NT // 4):
        steps += [("kv", t) for t in range(4 * c, 4 * c + 4)]
        if c:
            steps.append(("kT", c - 1))
    steps += [("q", 0), ("kT", NT // 4 - 1), ("qT", 0)]
    products, projections = [], []

    def finish(unit):
        steps.extend(("wo", u) for u in projections)
        steps.extend(("pv",) + p for p in products)
        products.clear()
        steps.append(("outT", unit))
        projections[:] = [unit]

    for i in range(NT + 1):
        for h in range(GH):
            scores = [("score", i, h, b) for b in range(len(score_blocks(i)))] if i < NT else []
            tiles = quarter(i, h)
            half = len(scores)
            if i >= 2 and 0 in tiles:
                half = (half + 1) // 2
                steps += scores[:half]
                finish(i - 2)
                steps += scores[half:]
            else:
                steps += scores
            for j in tiles:
                steps.append(("pT", i - 1, j))
                if j >= 1 and projections:
                    steps.append(("wo", projections.pop()))
                products.append((i - 1, j))
                if len(products) > LAG:
                    steps.append(("pv",) + products.pop(0))
            if h == 0 and i < NT - 1:
                steps.append(("q", i + 1))
            if h == 1 and i < NT - 1:
                steps.append(("q_sums", i + 1))
            if h == 2 and i < NT - 1:
                steps.append(("qT", i + 1))
            if i < NT:
                steps.append(("end", i, h))
    finish(NT - 1)
    return steps + [("wo", NT - 1)]


def scalar_steps():
    out, exps = [], []
    for step in group_steps():
        if step[0] == "score":
            exps.append(step)
        elif step[0] in ("q", "end"):
            out += exps + [step]
            exps = []
        else:
            out.append(step)
            if step[0] in ("pT", "qT") and exps:
                out.append(exps.pop(0))
    return out


def numbered(steps, kinds):
    found = [s for s in steps if s[0] in kinds]
    return {s: n for n, s in enumerate(found)}, len(found)


def block_kernel(nc, x, Wq, Wk, Wv, Wo, gq, gk, gate_w, up_w, down_w, gate_s, up_s, down_s, out):
    steps = group_steps()
    slot, slots = {}, 0
    for s in steps:
        if s[0] in ("kv", "q", "score"):
            slot[s] = slots
            slots += 1
    tslot, tslots = numbered(steps, ("kT", "qT", "pT", "wo"))
    last_counts = 1 + -tslots % TBANKS
    tslots += last_counts - 1
    hslot, hslots = numbered(steps, ("kT", "qT", "pT"))
    pv, pvs = numbered(steps, ("pv",))
    assert slots % 4 == 0 and tslots % TBANKS == 0 and pvs % PBUFS == 0 and NT % 2 == 0
    long_rows = [i for i in range(NT) if len(score_blocks(i)) > 1]
    T0 = PAIRS
    T1, H1 = T0 + GROUPS * tslots, T0 + GROUPS * hslots
    WT = 3 * (MT // 2)
    T2, H2 = T1 + WT, H1 + WT
    T3 = T2 + PAIRS

    ctx = ExitStack()
    with ctx:
        def sb(name, shape, dt):
            return ctx.enter_context(nc.sbuf_tensor(name, shape, dt))

        def sem(name):
            return ctx.enter_context(nc.semaphore(name))

        x1 = sb("x1", [P, NT * HID], fp32)
        normT_hi = sb("normT_hi", [P, CT, ROWS], fp32r)
        normT_lo = sb("normT_lo", [P, CT, ROWS], fp32r)
        w_raw = sb("w_raw", [P, WCOLS], fp32)
        w_hi = sb("w_hi", [P, WCOLS], fp32r)
        w_lo = sb("w_lo", [P, WCOLS], fp32r)
        kT_hi = sb("kT_hi", [P, ROWS], fp32r)
        kT_lo = sb("kT_lo", [P, ROWS], fp32r)
        v_hi = sb("v_hi", [P, NT * D], fp32r)
        v_lo = sb("v_lo", [P, NT * D], fp32r)
        q_rows = sb("q_rows", [P, QW], fp32)
        q_sqr = sb("q_sqr", [P, QW], fp32)
        qT_hi = sb("qT_hi", [P, 2, QW], fp32r)
        qT_lo = sb("qT_lo", [P, 2, QW], fp32r)
        probs = [sb("probs_even", [P, GH, (NT - 1) * P], fp32), sb("probs_odd", [P, GH, NT * P], fp32)]
        pT_hi = sb("pT_hi", [P, PBUFS, QW], fp32r)
        pT_lo = sb("pT_lo", [P, PBUFS, QW], fp32r)
        outT_hi = sb("outT_hi", [P, QW], fp32r)
        outT_lo = sb("outT_lo", [P, QW], fp32r)
        ident = sb("ident", [P, P], fp32)
        ident_b = sb("ident_b", [P, P], bf16)
        mask_b = sb("mask_b", [P, P], bf16)
        half_neg = sb("half_neg", [P, NT], fp32)
        bn = sb("bn", [P, NT, 6], fp32)
        mean_var = sb("mean_var", [P, NT, 2], fp32)
        rstd = sb("rstd", [P, NT], fp32)
        gain_q = sb("gain_q", [P, 1], fp32)
        gain_k = sb("gain_k", [P, 1], fp32)
        gain = sb("gain", [P, 1], fp32)
        k_ssq = sb("k_ssq", [P, NT], fp32)
        k_var = sb("k_var", [P, NT], fp32)
        k_rstd = sb("k_rstd", [P, NT], fp32)
        q_ssq = sb("q_ssq", [P, 2, GH], fp32)
        q_var = sb("q_var", [P, 2, GH], fp32)
        q_scale = sb("q_scale", [P, 2, GH], fp32)
        q_scale_neg = sb("q_scale_neg", [P, 2, GH], fp32)
        block_max = sb("block_max", [P, 2, GH, 4], fp32)
        scaled_max = sb("scaled_max", [P, 2, GH, 4], fp32)
        bias = sb("bias", [P, 2, GH], fp32)
        block_sum = sb("block_sum", [P, 2, GH, 4], fp32)
        row_sum = sb("row_sum", [P, 2, GH], fp32)
        row_inv = sb("row_inv", [P, 2, GH], fp32)
        gate_half = sb("gate_half", [P, MT], fp32)
        gate_col = sb("gate_col", [P, MT], fp32)
        up_col = sb("up_col", [P, MT], fp32)
        down_row = sb("down_row", [P, HID], fp32)

        spare = probs[1][:, :, :].rearrange("p h n -> p (h n)")
        rows = spare[:, 0:NT * HID].rearrange("p (t c) -> p t c", c=HID)
        kv_rows = rows
        ff = spare[:, NT * HID:NT * HID + 8 * CHUNK].rearrange("p (k a n) -> p k a n", k=4, a=2)
        ff_tanh, ff_gate, ff_part, ff_hidden = (ff[:, k, :, :] for k in range(4))
        y_part = q_sqr[:, :].rearrange("p (a n) -> p a n", a=2)
        raw = probs[0][:, :, :].rearrange("p h n -> p (h n)")
        squares = raw[:, 0:NT * D].rearrange("p (t d) -> p t d", d=D)
        gate_raw = raw[:, 0:MT * HID].rearrange("p (m c) -> p m c", c=HID)
        up_raw = raw[:, MT * HID:2 * MT * HID].rearrange("p (m c) -> p m c", c=HID)
        down_raw = raw[:, 2 * MT * HID:2 * MT * HID + CT * IPAD].rearrange("p (r i) -> p r i", i=IPAD)
        ffw = [(kT_hi, kT_lo), (v_hi, v_lo), (w_hi, w_lo)]

        slot_bank = [ctx.enter_context(nc.psum_tensor(f"slot{n}", [P, BANK], fp32)) for n in range(4)]
        tslot_bank = [ctx.enter_context(nc.psum_tensor(f"tslot{n}", [P, BANK], fp32)) for n in range(TBANKS)]
        outT_bank = ctx.enter_context(nc.psum_tensor("outT", [P, BANK], fp32))
        down_bank = tslot_bank + [outT_bank]

        x_in = [sem(f"x_in{c}") for c in range(4)]
        gains_in = sem("gains_in")
        ff_scales_in = sem("ff_scales_in")
        ffw_in = sem("ffw_in")
        w_in = sem("w_in")
        y_out = sem("y_out")
        consts = sem("consts")
        pool_waits = sem("pool_waits")
        ident_zero = sem("ident_zero")
        gains_ready = sem("gains_ready")
        pads_ready = sem("pads_ready")
        bn_done = sem("bn_done")
        aggr_done = sem("aggr_done")
        var_done = sem("var_done")
        rstd_ready = sem("rstd_ready")
        norm_ready = sem("norm_ready")
        w_hi_done = sem("w_hi_done")
        w_split = sem("w_split")
        slot_full = sem("slot_full")
        slot_free = sem("slot_free")
        t_full = sem("t_full")
        t_hi = sem("t_hi")
        t_free = sem("t_free")
        k_var_done = sem("k_var_done")
        k_rstd_ready = sem("k_rstd_ready")
        k_normed = sem("k_normed")
        v_hi_done = sem("v_hi_done")
        v_ready = sem("v_ready")
        q_sqr_done = sem("q_sqr_done")
        q_ssq_done = sem("q_ssq_done")
        q_var_done = sem("q_var_done")
        q_root_done = sem("q_root_done")
        q_scale_ready = sem("q_scale_ready")
        max_done = sem("max_done")
        bias_ready = sem("bias_ready")
        sum_done = sem("sum_done")
        inv_ready = sem("inv_ready")
        probs_ready = sem("probs_ready")
        pv_done = sem("pv_done")
        out_hi = sem("out_hi")
        out_ready = sem("out_ready")
        gate_full = sem("gate_full")
        up_full = sem("up_full")
        gate_read = sem("gate_read")
        up_read = sem("up_read")
        ff_part_done = sem("ff_part_done")
        ff_hi = sem("ff_hi")
        ff_ready = sem("ff_ready")
        down_step = sem("down_step")
        down_read = sem("down_read")
        y_scaled = sem("y_scaled")
        y_ready = sem("y_ready")

        block = ctx.enter_context(nc.Block())

        @block.sync
        def _(sp):
            xv = x[0].rearrange("(k t p) c -> k p t c", p=P, t=TPC)
            x1v = x1[:, :].rearrange("p (k t c) -> p k t c", k=4, c=HID)
            for c in range(4):
                sp.dma_start(x1v[:, c, :, :], xv[c]).then_inc(x_in[c], 16)
            with sp.Fori(0, GROUPS) as g:
                sp.wait_ge(w_split, 3 * g + 1)
                wkv = w_raw[:, WKV0:WO0].rearrange("p (c n) -> p c n", c=CT)
                sp.dma_start(wkv[:, :, 0:D], Wk.rearrange("(c p) n -> p c n", p=P)[:, :, bass.ds(g * D, D)]).then_inc(w_in, 16)
                sp.dma_start(wkv[:, :, D:2 * D], Wv.rearrange("(c p) n -> p c n", p=P)[:, :, bass.ds(g * D, D)]).then_inc(w_in, 16)
                sp.dma_start(w_raw[:, WQ0:WKV0].rearrange("p (c n) -> p c n", c=CT),
                             Wq.rearrange("(c p) n -> p c n", p=P)[:, :, bass.ds(g * QW, QW)]).then_inc(w_in, 16)
                sp.dma_start(w_raw[:, WO0:WCOLS].rearrange("p (h n) -> p h n", h=GH),
                             Wo.rearrange("(g h p) n -> g p h n", h=GH, p=P)[bass.ds(g, 1), :, :, :].rearrange("g p h n -> (g p) h n")).then_inc(w_in, 16)
            last_even = tslot[("pT", NT - 2, NT - 2)]
            sp.wait_ge(t_full, T0 + (GROUPS - 1) * tslots + last_even + 1)
            full = MT - 1
            for src, dst in ((gate_w, gate_raw), (up_w, up_raw)):
                sp.dma_start(dst[:, 0:full, :], src[0:full * P, :].rearrange("(m p) c -> p m c", p=P)).then_inc(ffw_in, 16)
                sp.dma_start(dst[0:INTER - full * P, full, :], src[full * P:INTER, :]).then_inc(ffw_in, 16)
            sp.dma_start(down_raw[:, :, 0:INTER], down_w.rearrange("(r p) i -> p r i", p=P)).then_inc(ffw_in, 16)
            with sp.Fori(0, NCH) as k:
                outv = out[0].rearrange("(k t p) c -> k p t c", p=P, t=TPC)
                for t in range(TPC):
                    sp.wait_ge(y_ready, k * TPC + t + 1)
                    sp.dma_start(outv[bass.ds(k, 1), :, t, :].rearrange("k p c -> (k p) c"),
                                 x1[:, bass.ds(k * (TPC * HID) + t * HID, HID)]).then_inc(y_out, 16)
            sp.wait_ge(y_out, 16 * NT)

        @block.gpsimd
        def _(pool):
            nc.gpsimd.memset(half_neg[:, :], -0.5).then_inc(consts, 1)
            nc.gpsimd.memset(ident[:, :], 0.0).then_inc(ident_zero, 1)
            nc.gpsimd.memset(mask_b[:, :], 0.0).then_inc(ident_zero, 1)
            pool.wait_ge(ident_zero, 2)
            nc.gpsimd.affine_select(out=ident[:, :], in_=ident[:, :], compare_op=ALU.not_equal, fill=1.0,
                                    base=0, pattern=[[-1, P]], channel_multiplier=1).then_inc(consts, 1)
            nc.gpsimd.affine_select(out=mask_b[:, :], in_=mask_b[:, :], compare_op=ALU.is_ge, fill=MASKED,
                                    base=0, pattern=[[-1, P]], channel_multiplier=1).then_inc(consts, 1)
            pool.wait_ge(consts, 3)
            nc.gpsimd.tensor_copy(ident_b[:, :], ident[:, :]).then_inc(consts, 1)

            def layernorm_roots(n):
                for c in range(4):
                    t = slice(4 * c, 4 * c + 4)
                    pool.wait_ge(aggr_done, n * NT + 4 * c + 4)
                    nc.gpsimd.tensor_scalar(rstd[:, t], mean_var[:, t, 1], 1.0, LN_EPS,
                                            ALU.mult, ALU.add).then_inc(var_done, 1)
                    pool.wait_ge(var_done, n * 4 + c + 1)
                    nc.gpsimd.tensor_tensor(rstd[:, t], rstd[:, t], half_neg[:, t], ALU.pow).then_inc(rstd_ready, 1)

            layernorm_roots(0)

            def wait_for(semaphore, value):
                pool.wait_ge(semaphore, value)
                pool.sem_inc(pool_waits, 1)

            def query_square(g, i):
                wait_for(slot_free, 4 + g * slots + slot[("q", i)] + 1)
                nc.gpsimd.tensor_tensor(q_sqr[:, :], q_rows[:, :], q_rows[:, :], ALU.mult).then_inc(q_sqr_done, 1)

            def query_scale(g, i):
                a = i % 2
                wait_for(q_ssq_done, g * NT + i + 1)
                nc.gpsimd.tensor_scalar(q_var[:, a, :], q_ssq[:, a, :], 1.0, D * RMS_EPS,
                                        ALU.mult, ALU.add).then_inc(q_var_done, 1)
                wait_for(q_var_done, g * NT + i + 1)
                nc.gpsimd.tensor_tensor(q_scale[:, a, :], q_var[:, a, :], half_neg[:, 0:GH], ALU.pow).then_inc(q_root_done, 1)
                wait_for(q_root_done, g * NT + i + 1)
                nc.gpsimd.tensor_scalar(q_scale_neg[:, a, :], q_scale[:, a, :], -1.0, 1.0,
                                        ALU.mult, ALU.mult).then_inc(q_scale_ready, 1)

            with pool.Fori(0, GROUPS) as g:
                for step in steps:
                    if step[0] == "kv" and step[1] % 4 == 3:
                        c = step[1] // 4
                        t = slice(4 * c, 4 * c + 4)
                        wait_for(slot_free, 4 + g * slots + slot[step] + 1)
                        nc.gpsimd.tensor_scalar(k_var[:, t], k_ssq[:, t], 1.0 / D, RMS_EPS,
                                                ALU.mult, ALU.add).then_inc(k_var_done, 1)
                        wait_for(k_var_done, g * 4 + c + 1)
                        nc.gpsimd.tensor_tensor(k_rstd[:, t], k_var[:, t], half_neg[:, t], ALU.pow).then_inc(k_rstd_ready, 1)
                        nc.gpsimd.tensor_copy(v_hi[:, 4 * c * D:(4 * c + 4) * D].rearrange("p (t d) -> p t d", d=D),
                                              kv_rows[:, t, D:2 * D]).then_inc(v_hi_done, 1)
                    elif step[0] == "q" and step[1] == 0:
                        query_square(g, 0)
                        query_scale(g, 0)
                    elif step[0] == "end" and step[1] < NT:
                        _, i, h = step
                        if i + 1 < NT and h == 0:
                            query_square(g, i + 1)
                        wait_for(inv_ready, g * NT * GH + i * GH + h + 1)
                        row = probs[i % 2][:, h, 0:(i + 1) * P]
                        nc.gpsimd.tensor_scalar(row, row, row_inv[:, i % 2, h:h + 1], 1.0,
                                                ALU.mult, ALU.mult).then_inc(probs_ready, 1)
                        if i + 1 < NT and h == 1:
                            query_scale(g, i + 1)

            layernorm_roots(1)

        @block.scalar
        def _(act):
            act.sem_inc(slot_free, 4)
            act.sem_inc(gate_read, 2)
            for dst, src in ((gain_q, gq), (gain_k, gk)):
                act.dma_start(dst[:, :], src.rearrange("(p a) -> p a", a=1)).then_inc(gains_in, 16)
            full = MT - 1
            act.wait_ge(pads_ready, 2)
            for dst, src in ((gate_col, gate_s), (up_col, up_s)):
                act.dma_start(dst[:, 0:full], src[0:full * P].rearrange("(m p) -> p m", p=P),
                              allow_slow_non_contiguous=True).then_inc(ff_scales_in, 16)
                act.dma_start(dst[0:INTER - full * P, full:MT],
                              src[full * P:INTER].rearrange("(p a) -> p a", a=1)).then_inc(ff_scales_in, 16)
            act.dma_start(down_row[:, :], down_s.partition_broadcast(P)).then_inc(ff_scales_in, 16)

            def layernorm_hi(tbase, hbase):
                for r in range(PAIRS):
                    act.wait_ge(t_full, tbase + r + 1)
                    nc.scalar.activation(normT_hi[:, :, 2 * r * P:2 * (r + 1) * P],
                                         tslot_bank[(tbase + r) % TBANKS][:, :].rearrange("p (c n) -> p c n", c=CT),
                                         ACT.Copy).then_inc(t_hi, 1)

            layernorm_hi(0, 0)

            with act.Fori(0, GROUPS) as g:
                act.wait_ge(w_in, 64 * g + 64)
                act.wait_ge(t_full, T0 + g * tslots)
                for a, b in ((WKV0, WO0), (WQ0, WKV0), (WO0, WCOLS)):
                    nc.scalar.activation(w_hi[:, a:b], w_raw[:, a:b], ACT.Copy).then_inc(w_hi_done, 1)
                for step in scalar_steps():
                    if step[0] == "kv":
                        t = step[1]
                        src = slot_bank[slot[step] % 4]
                        act.wait_ge(slot_full, g * slots + slot[step] + 1)
                        nc.scalar.activation(squares[:, t, :], src[:, 0:D], ACT.Square, accum_out=k_ssq[:, t:t + 1])
                        nc.scalar.activation(kv_rows[:, t, :], src[:, 0:2 * D], ACT.Copy).then_inc(slot_free, 1)
                    elif step[0] == "kT":
                        c = step[1]
                        act.wait_ge(t_full, T0 + g * tslots + tslot[step] + 1)
                        nc.scalar.activation(kT_hi[:, c * BANK:(c + 1) * BANK], tslot_bank[(T0 + tslot[step]) % TBANKS][:, :],
                                             ACT.Copy, scale=gain[:, 0:1]).then_inc(t_hi, 1)
                    elif step[0] == "q":
                        act.wait_ge(slot_full, g * slots + slot[step] + 1)
                        nc.scalar.activation(q_rows[:, :], slot_bank[slot[step] % 4][:, :], ACT.Copy).then_inc(slot_free, 1)
                    elif step[0] == "qT":
                        act.wait_ge(t_full, T0 + g * tslots + tslot[step] + 1)
                        nc.scalar.activation(qT_hi[:, step[1] % 2, :], tslot_bank[(T0 + tslot[step]) % TBANKS][:, :],
                                             ACT.Copy).then_inc(t_hi, 1)
                    elif step[0] == "score":
                        _, i, h, b = step
                        start, width = score_blocks(i)[b]
                        s = slot[step]
                        if b == 0:
                            act.wait_ge(bias_ready, g * NT * GH + i * GH + h + 1)
                        nc.scalar.activation(probs[i % 2][:, h, start:start + width], slot_bank[s % 4][:, 0:width], ACT.Exp,
                                             bias=bias[:, i % 2, h:h + 1], scale=q_scale[:, i % 2, h:h + 1],
                                             accum_out=block_sum[:, i % 2, h, b:b + 1]).then_inc(slot_free, 1)
                    elif step[0] == "pT":
                        n = pv[("pv",) + step[1:]]
                        act.wait_ge(t_full, T0 + g * tslots + tslot[step] + 1)
                        act.wait_ge(pv_done, g * pvs + n + 1)
                        nc.scalar.activation(pT_hi[:, n % PBUFS, :], tslot_bank[(T0 + tslot[step]) % TBANKS][:, :], ACT.Copy).then_inc(t_hi, 1)
                    elif step[0] == "outT":
                        i = step[1]
                        act.wait_ge(pv_done, PBUFS + g * pvs + pv[("pv", i, i)] + 1)
                        nc.scalar.activation(outT_hi[:, :], outT_bank[:, :], ACT.Copy).then_inc(out_hi, 1)

            for n in range(WT):
                act.wait_ge(t_full, T1 + n + 1)
                hi, m = ffw[n // (MT // 2)][0], n % (MT // 2)
                src = tslot_bank[(T1 + n) % TBANKS][:, :]
                if n // (MT // 2) < 2:
                    dst = hi[:, 0:CT * IPAD].rearrange("p (c i) -> p c i", c=CT)[:, :, 2 * m * P:2 * (m + 1) * P]
                    src = src.rearrange("p (c n) -> p c n", c=CT)
                else:
                    dst = hi[:, m * BANK:(m + 1) * BANK]
                nc.scalar.activation(dst, src, ACT.Copy).then_inc(t_hi, 1)
            layernorm_hi(T2, H2)

            with act.Fori(0, NCH) as k:
                for m in range(MT + 1):
                    if m < MT:
                        a = m % 2
                        g_bank = slot_bank[2 * a]
                        act.wait_ge(gate_full, k * MT + m + 1)
                        nc.scalar.activation(ff_tanh[:, a, :], g_bank[:, :], ACT.Tanh, scale=gate_half[:, m:m + 1])
                        nc.scalar.activation(ff_gate[:, a, :], g_bank[:, :], ACT.Copy,
                                             scale=gate_half[:, m:m + 1]).then_inc(gate_read, 1)
                    if m:
                        a = (m - 1) % 2
                        act.wait_ge(up_read, 2 + k * MT + m)
                        act.wait_ge(down_step, k * MT + m)
                        nc.scalar.activation(pT_hi[:, a, :], ff_hidden[:, a, :], ACT.Copy).then_inc(ff_hi, 1)

        @block.vector
        def _(dve):
            dve.sem_inc(w_split, 1)
            dve.sem_inc(t_free, TBANKS)
            dve.sem_inc(out_ready, 1)
            dve.sem_inc(up_read, 2)
            dve.sem_inc(down_read, 4)
            nc.vector.memset(gate_col[:, :], 0.0).then_inc(pads_ready, 1)
            nc.vector.memset(up_col[:, :], 0.0).then_inc(pads_ready, 1)

            def layernorm_rows(n, arrived):
                for c in range(4):
                    arrived(c)
                    for t in range(4 * c, 4 * c + 4):
                        nc.vector.bn_stats(bn[:, t, :], x1[:, t * HID:(t + 1) * HID]).then_inc(bn_done, 1)
                    for t in range(4 * c, 4 * c + 4):
                        dve.wait_ge(bn_done, n * NT + t + 1)
                        nc.vector.bn_aggr(mean_var[:, t, :], bn[:, t, :]).then_inc(aggr_done, 1)
                for c in range(4):
                    dve.wait_ge(rstd_ready, n * 4 + c + 1)
                    for t in range(4 * c, 4 * c + 4):
                        nc.vector.tensor_scalar(rows[:, t, :], x1[:, t * HID:(t + 1) * HID], mean_var[:, t, 0:1],
                                                rstd[:, t:t + 1], ALU.subtract, ALU.mult).then_inc(norm_ready, 1)

            def layernorm_lo(tbase, hbase):
                for r in range(PAIRS):
                    dve.wait_ge(t_hi, hbase + r + 1)
                    cols = slice(2 * r * P, 2 * (r + 1) * P)
                    nc.vector.tensor_tensor(normT_lo[:, :, cols],
                                            tslot_bank[(tbase + r) % TBANKS][:, :].rearrange("p (c n) -> p c n", c=CT),
                                            normT_hi[:, :, cols].bitcast(fp32), ALU.subtract).then_inc(t_free, 1)

            layernorm_rows(0, lambda c: dve.wait_ge(x_in[c], 16))
            layernorm_lo(0, 0)
            dve.wait_ge(gains_in, 16 * 2)
            nc.vector.tensor_tensor(gain[:, :], gain_q[:, :], gain_k[:, :], ALU.mult).then_inc(gains_ready, 1)

            def query_sums(g, i):
                dve.wait_ge(q_sqr_done, g * NT + i + 1)
                nc.vector.reduce_sum(q_ssq[:, i % 2, :], q_sqr[:, :].rearrange("p (h d) -> p h d", d=D),
                                     AX.X).then_inc(q_ssq_done, 1)

            def row_inverse(g, i, h):
                a, nb = i % 2, len(score_blocks(i))
                dve.wait_ge(slot_free, 4 + g * slots + slot[("score", i, h, nb - 1)] + 1)
                total = block_sum[:, a, h, 0:1]
                if nb > 1:
                    nc.vector.reduce_sum(row_sum[:, a, h:h + 1], block_sum[:, a, h, 0:nb], AX.X).then_inc(sum_done, 1)
                    dve.wait_ge(sum_done, g * GH * len(long_rows) + GH * long_rows.index(i) + h + 1)
                    total = row_sum[:, a, h:h + 1]
                nc.vector.reciprocal(row_inv[:, a, h:h + 1], total).then_inc(inv_ready, 1)

            rows_due = []

            with dve.Fori(0, GROUPS) as g:
                for n, (a, b) in enumerate(((WKV0, WO0), (WQ0, WKV0), (WO0, WCOLS))):
                    dve.wait_ge(w_hi_done, 3 * g + n + 1)
                    nc.vector.tensor_tensor(w_lo[:, a:b], w_raw[:, a:b], w_hi[:, a:b].bitcast(fp32),
                                            ALU.subtract).then_inc(w_split, 1)
                for step in steps:
                    if step[0] == "kv" and step[1] % 4 == 3:
                        c = step[1] // 4
                        dve.wait_ge(k_rstd_ready, 4 * g + c + 1)
                        for t in range(4 * c, 4 * c + 4):
                            nc.vector.tensor_scalar(kv_rows[:, t, 0:D], kv_rows[:, t, 0:D], k_rstd[:, t:t + 1], None,
                                                    ALU.mult).then_inc(k_normed, 1)
                        dve.wait_ge(v_hi_done, 4 * g + c + 1)
                        cols = slice(4 * c * D, (4 * c + 4) * D)
                        nc.vector.tensor_tensor(v_lo[:, cols].rearrange("p (t d) -> p t d", d=D),
                                                kv_rows[:, 4 * c:4 * c + 4, D:2 * D],
                                                v_hi[:, cols].bitcast(fp32).rearrange("p (t d) -> p t d", d=D),
                                                ALU.subtract).then_inc(v_ready, 1)
                    elif step[0] == "kT":
                        c = step[1]
                        dve.wait_ge(t_hi, T0 + g * hslots + hslot[step] + 1)
                        nc.vector.scalar_tensor_tensor(out=kT_lo[:, c * BANK:(c + 1) * BANK],
                                                       in0=tslot_bank[(T0 + tslot[step]) % TBANKS][:, :], scalar=gain[:, 0:1],
                                                       in1=kT_hi[:, c * BANK:(c + 1) * BANK].bitcast(fp32),
                                                       op0=ALU.mult, op1=ALU.subtract).then_inc(t_free, 1)
                    elif step[0] == "qT":
                        a = step[1] % 2
                        dve.wait_ge(t_hi, T0 + g * hslots + hslot[step] + 1)
                        nc.vector.tensor_tensor(qT_lo[:, a, :], tslot_bank[(T0 + tslot[step]) % TBANKS][:, :],
                                                qT_hi[:, a, :].bitcast(fp32), ALU.subtract).then_inc(t_free, 1)
                    elif step[0] == "score":
                        _, i, h, b = step
                        a, blocks = i % 2, score_blocks(i)
                        dve.wait_ge(slot_full, g * slots + slot[step] + 1)
                        nc.vector.tensor_reduce(block_max[:, a, h, b:b + 1], slot_bank[slot[step] % 4][:, 0:blocks[b][1]],
                                                AX.X, ALU.max).then_inc(max_done, 1)
                        if b == 0 and rows_due:
                            row_inverse(g, *rows_due.pop())
                        if b == len(blocks) - 1:
                            if h == 0:
                                dve.wait_ge(q_scale_ready, g * NT + i + 1)
                            done = sum(GH * len(score_blocks(u)) for u in range(i)) + (h + 1) * len(blocks)
                            dve.wait_ge(max_done, g * (slots - 2 * NT) + done)
                            nc.vector.tensor_scalar(scaled_max[:, a, h, 0:len(blocks)], block_max[:, a, h, 0:len(blocks)],
                                                    q_scale_neg[:, a, h:h + 1], None, ALU.mult, ALU.min,
                                                    accum_out=bias[:, a, h:h + 1]).then_inc(bias_ready, 1)
                            rows_due.append((i, h))
                    elif step[0] == "pT":
                        n = pv[("pv",) + step[1:]]
                        if step[1] == NT - 1 and rows_due:
                            row_inverse(g, *rows_due.pop())
                        dve.wait_ge(t_hi, T0 + g * hslots + hslot[step] + 1)
                        nc.vector.tensor_tensor(pT_lo[:, n % PBUFS, :], tslot_bank[(T0 + tslot[step]) % TBANKS][:, :],
                                                pT_hi[:, n % PBUFS, :].bitcast(fp32), ALU.subtract).then_inc(t_free, 1)
                    elif step[0] == "outT":
                        i = step[1]
                        dve.wait_ge(out_hi, g * NT + i + 1)
                        nc.vector.tensor_tensor(outT_lo[:, :], outT_bank[:, :], outT_hi[:, :].bitcast(fp32),
                                                ALU.subtract).then_inc(out_ready, 1)
                    elif step[0] == "wo":
                        i = step[1]
                        dve.wait_ge(t_full, T0 + g * tslots + tslot[step] + 1)
                        cols = slice(i * HID, (i + 1) * HID)
                        nc.vector.tensor_tensor(x1[:, cols], tslot_bank[(T0 + tslot[step]) % TBANKS][:, 0:HID], x1[:, cols],
                                                ALU.add).then_inc(t_free, last_counts if i == NT - 1 else 1)
                    elif step[0] == "q_sums":
                        query_sums(g, step[1])
                    elif step == ("q", 0):
                        query_sums(g, 0)

            dve.wait_ge(ff_scales_in, 16 * 5)
            nc.vector.tensor_scalar(gate_half[:, :], gate_col[:, :], 0.5, None, ALU.mult).then_inc(gains_ready, 1)
            dve.wait_ge(t_free, TBANKS + T1)
            full = MT - 1
            nc.vector.memset(gate_raw[64:P, full, :], 0.0).then_inc(pads_ready, 1)
            nc.vector.memset(up_raw[64:P, full, :], 0.0).then_inc(pads_ready, 1)
            nc.vector.memset(down_raw[:, :, INTER:IPAD], 0.0).then_inc(pads_ready, 1)
            layernorm_rows(1, lambda c: None)
            for n in range(WT):
                dve.wait_ge(t_hi, H1 + n + 1)
                (hi, lo), m = ffw[n // (MT // 2)], n % (MT // 2)
                src = tslot_bank[(T1 + n) % TBANKS][:, :]
                if n // (MT // 2) < 2:
                    cols = slice(2 * m * P, 2 * (m + 1) * P)
                    hi = hi[:, 0:CT * IPAD].bitcast(fp32).rearrange("p (c i) -> p c i", c=CT)[:, :, cols]
                    lo = lo[:, 0:CT * IPAD].rearrange("p (c i) -> p c i", c=CT)[:, :, cols]
                    src = src.rearrange("p (c n) -> p c n", c=CT)
                else:
                    hi, lo = hi[:, m * BANK:(m + 1) * BANK].bitcast(fp32), lo[:, m * BANK:(m + 1) * BANK]
                nc.vector.tensor_tensor(lo, src, hi, ALU.subtract).then_inc(t_free, 1)
            layernorm_lo(T2, H2)

            with dve.Fori(0, NCH) as k:
                for m in range(MT):
                    a = m % 2
                    dve.wait_ge(gate_read, 2 + k * MT + m + 1)
                    nc.vector.scalar_tensor_tensor(out=ff_part[:, a, :], in0=ff_tanh[:, a, :], scalar=1.0,
                                                   in1=ff_gate[:, a, :], op0=ALU.add, op1=ALU.mult).then_inc(ff_part_done, 1)
                    dve.wait_ge(ff_part_done, k * MT + m + 1)
                    dve.wait_ge(up_full, k * MT + m + 1)
                    nc.vector.scalar_tensor_tensor(out=ff_hidden[:, a, :], in0=slot_bank[2 * a + 1][:, :],
                                                   scalar=up_col[:, m:m + 1], in1=ff_part[:, a, :],
                                                   op0=ALU.mult, op1=ALU.mult).then_inc(up_read, 1)
                    dve.wait_ge(ff_hi, k * MT + m + 1)
                    nc.vector.tensor_tensor(pT_lo[:, a, :], ff_hidden[:, a, :], pT_hi[:, a, :].bitcast(fp32),
                                            ALU.subtract).then_inc(ff_ready, 1)
                dve.wait_ge(down_step, 2 + k * MT + MT)
                for t in range(TPC):
                    nc.vector.tensor_tensor(y_part[:, t % 2, :], down_bank[t][:, 0:HID], down_row[:, :],
                                            ALU.mult).then_inc(down_read, 1)
                    cols = bass.ds(k * (TPC * HID) + t * HID, HID)
                    dve.wait_ge(down_read, 4 + k * TPC + t + 1)
                    nc.vector.tensor_tensor(x1[:, cols], y_part[:, t % 2, :], x1[:, cols], ALU.add).then_inc(y_ready, 1)

        @block.tensor
        def _(pe):
            pe.sem_inc(pv_done, PBUFS)
            pe.sem_inc(down_step, 2)

            def product3(bank, hi_l, lo_l, hi_r, lo_r, start, stop, masked=None):
                for n, (l, r) in enumerate(((hi_l, hi_r), (lo_l, hi_r), (hi_l, lo_r))):
                    last = nc.tensor.matmul(bank, l, r, start=start and n == 0, stop=stop and n == 2)
                    if n == 0 and masked is not None:
                        nc.tensor.matmul(masked, ident_b[:, :], mask_b[:, :], start=False, stop=False)
                return last

            def layernorm_transpose(n, tbase):
                for r in range(PAIRS):
                    pe.wait_ge(norm_ready, n * NT + 2 * r + 2)
                    pe.wait_ge(t_free, tbase + r + 1)
                    for c in range(CT):
                        for t in range(2):
                            at = (2 * c + t) * P
                            last = nc.tensor.transpose(tslot_bank[(tbase + r) % TBANKS][:, at:at + P],
                                                       rows[:, 2 * r + t, c * P:(c + 1) * P], ident[:, :])
                    last.then_inc(t_full, 1)

            pe.wait_ge(consts, 4)
            layernorm_transpose(0, 0)
            pe.wait_ge(t_free, TBANKS + T0)

            with pe.Fori(0, GROUPS) as g:
                for step in steps:
                    if step[0] in ("kv", "q"):
                        t = step[1]
                        if t == 0:
                            pe.wait_ge(w_split, 3 * g + (2 if step[0] == "kv" else 3))
                        pe.wait_ge(slot_free, g * slots + slot[step] + 1)
                        at, width = (WKV0, 2 * D) if step[0] == "kv" else (WQ0, QW)
                        for c in range(CT):
                            w = slice(at + c * width, at + (c + 1) * width)
                            last = product3(slot_bank[slot[step] % 4][:, 0:width],
                                            normT_hi[:, c, t * P:(t + 1) * P], normT_lo[:, c, t * P:(t + 1) * P],
                                            w_hi[:, w], w_lo[:, w], start=(c == 0), stop=(c == CT - 1))
                        last.then_inc(slot_full, 1)
                    elif step[0] in ("kT", "qT", "pT"):
                        if step[0] == "kT":
                            pe.wait_ge(k_normed, g * NT + 4 * step[1] + 4)
                            tiles = [kv_rows[:, 4 * step[1] + t, 0:D] for t in range(4)]
                        elif step[0] == "qT":
                            pe.wait_ge(slot_free, 4 + g * slots + slot[("q", step[1])] + 1)
                            tiles = [q_rows[:, h * D:(h + 1) * D] for h in range(GH)]
                        else:
                            _, i, j = step
                            if j == 0:
                                pe.wait_ge(probs_ready, g * NT * GH + (i + 1) * GH)
                            tiles = [probs[i % 2][:, h, j * P:(j + 1) * P] for h in range(GH)]
                        pe.wait_ge(t_free, T0 + g * tslots + tslot[step] + 1)
                        for n, tile in enumerate(tiles):
                            last = nc.tensor.transpose(tslot_bank[(T0 + tslot[step]) % TBANKS][:, n * P:(n + 1) * P], tile, ident[:, :])
                        last.then_inc(t_full, 1)
                    elif step[0] == "score":
                        _, i, h, b = step
                        start, width = score_blocks(i)[b]
                        diagonal = start + width == (i + 1) * P
                        if h == 0 and b == 0:
                            pe.wait_ge(t_free, TBANKS + T0 + g * tslots + tslot[("qT", i)] + 1)
                        bank = slot_bank[slot[step] % 4]
                        q = slice(h * D, (h + 1) * D)
                        cols = slice(start, start + max(width, 2 * P))
                        pe.wait_ge(slot_free, g * slots + slot[step] + 1)
                        product3(bank[:, 0:max(width, 2 * P)], qT_hi[:, i % 2, q], qT_lo[:, i % 2, q],
                                 kT_hi[:, cols], kT_lo[:, cols], start=True, stop=True,
                                 masked=bank[:, width - P:width] if diagonal else None).then_inc(slot_full, 1)
                    elif step[0] == "pv":
                        _, i, j = step
                        n = pv[step]
                        if (i, j) == (0, 0):
                            pe.wait_ge(v_ready, 4 * g + 4)
                        if j == 0:
                            pe.wait_ge(out_ready, g * NT + i + 1)
                        pe.wait_ge(t_free, TBANKS + T0 + g * tslots + tslot[("pT", i, j)] + 1)
                        product3(outT_bank[:, :], v_hi[:, j * D:(j + 1) * D], v_lo[:, j * D:(j + 1) * D],
                                 pT_hi[:, n % PBUFS, :], pT_lo[:, n % PBUFS, :], start=(j == 0), stop=(j == i)).then_inc(pv_done, 1)
                    elif step[0] == "wo":
                        i = step[1]
                        if i == 0:
                            pe.wait_ge(w_split, 3 * g + 4)
                        pe.wait_ge(out_ready, 1 + g * NT + i + 1)
                        pe.wait_ge(t_free, T0 + g * tslots + tslot[step] + 1)
                        for h in range(GH):
                            o = slice(h * D, (h + 1) * D)
                            w = slice(WO0 + h * HID, WO0 + (h + 1) * HID)
                            last = product3(tslot_bank[(T0 + tslot[step]) % TBANKS][:, 0:HID], outT_hi[:, o], outT_lo[:, o],
                                            w_hi[:, w], w_lo[:, w], start=(h == 0), stop=(h == GH - 1))
                        last.then_inc(t_full, last_counts if i == NT - 1 else 1)

            pe.wait_ge(ffw_in, 16 * 5)
            pe.wait_ge(pads_ready, 5)
            for n in range(WT):
                m = n % (MT // 2)
                pe.wait_ge(t_free, T1 + n + 1)
                for a in range(2):
                    for b in range(2):
                        if n // (MT // 2) < 2:
                            tile = (gate_raw, up_raw)[n // (MT // 2)][:, 2 * m + b, a * P:(a + 1) * P]
                        else:
                            tile = down_raw[:, b, (2 * m + a) * P:(2 * m + a + 1) * P]
                        at = (2 * a + b) * P
                        last = nc.tensor.transpose(tslot_bank[(T1 + n) % TBANKS][:, at:at + P], tile, ident[:, :])
                last.then_inc(t_full, 1)
            layernorm_transpose(1, T2)
            pe.wait_ge(t_free, TBANKS + T3)

            with pe.Fori(0, NCH) as k:
                for m in range(MT + 1):
                    if m < MT:
                        a = m % 2
                        for bank, (hi, lo), read, full in ((slot_bank[2 * a], ffw[0], gate_read, gate_full),
                                                           (slot_bank[2 * a + 1], ffw[1], up_read, up_full)):
                            pe.wait_ge(read, k * MT + m + 1)
                            for c in range(CT):
                                w = slice(c * IPAD + m * P, c * IPAD + (m + 1) * P)
                                cols = bass.ds(k * CHUNK, CHUNK)
                                last = product3(bank[:, :], hi[:, w], lo[:, w], normT_hi[:, c, cols], normT_lo[:, c, cols],
                                                start=(c == 0), stop=(c == CT - 1))
                            last.then_inc(full, 1)
                    if m:
                        a = (m - 1) % 2
                        hi, lo = ffw[2]
                        w = slice((m - 1) * HID, m * HID)
                        pe.wait_ge(ff_ready, k * MT + m)
                        for t in range(TPC):
                            if m == 1:
                                pe.wait_ge(down_read, k * TPC + t + 1)
                            r = slice(t * P, (t + 1) * P)
                            last = product3(down_bank[t][:, 0:HID], pT_hi[:, a, r], pT_lo[:, a, r], hi[:, w], lo[:, w],
                                            start=(m == 1), stop=(m == MT))
                        last.then_inc(down_step, 1)


_INS = ["L0_attn_x", "L0_attn_Wq", "L0_attn_Wk", "L0_attn_Wv", "L0_attn_Wo", "L0_attn_gq", "L0_attn_gk",
        "L0_ffn_gate_w", "L0_ffn_up_w", "L0_ffn_down_w", "L0_ffn_gate_s", "L0_ffn_up_s", "L0_ffn_down_s"]
_OUT = ((1, ROWS, HID), "float32")


def kernel(**inputs):
    import numpy as _np
    import concourse.bacc as _bacc
    from concourse import mybir as _mybir
    from concourse.bass_utils import run_bass_kernel_spmd as _run

    nc = _bacc.Bacc("TRN2", target_bir_lowering=False, num_devices=1)
    arrays, args = {}, []
    for name in _INS:
        a = _np.ascontiguousarray(inputs[name])
        arrays[f"in_{name}_dram"] = a
        args.append(nc.dram_tensor(f"in_{name}_dram", a.shape, _mybir.dt.from_np(a.dtype), kind="ExternalInput").ap())
    args.append(nc.dram_tensor("out_dram", _OUT[0], _mybir.dt.from_np(_np.dtype(_OUT[1])), kind="ExternalOutput").ap())
    block_kernel(nc, *args)
    r = _run(nc, [arrays], core_ids=[0])
    return r.results[0]["out_dram"]
```

```python
from contextlib import ExitStack

import concourse.bass as bass
from concourse import mybir

fp32 = mybir.dt.float32
fp32r = mybir.dt.float32r
bf16 = mybir.dt.bfloat16
ALU = mybir.AluOpType
ACT = mybir.ActivationFunctionType
AX = mybir.AxisListType

P = 128
ROWS = 2048
HID = 256
HEADS = 16
GROUPS = 4
GH = HEADS // GROUPS
D = 128
INTER = 704
BANK = 512
RMS_EPS = 1e-6
LN_EPS = 1e-5
MASKED = -1e30

NT = ROWS // P
CT = HID // P
QW = GH * D
MT = -(-INTER // P)
IPAD = MT * P
CHUNK = BANK
NCH = ROWS // CHUNK
TPC = CHUNK // P
PAIRS = NT // 2
LAG = 2
TBANKS = 3
PBUFS = 4
WQ0, WKV0, WO0 = 0, CT * QW, CT * QW + CT * 2 * D
WCOLS = WO0 + GH * HID
W_PARTS = ((WKV0, WO0), (WQ0, WKV0), (WO0, WCOLS))


def score_blocks(i):
    n = (i + 1) * P
    return [(b, min(BANK, n - b)) for b in range(0, n, BANK)]


def quarter(n, h):
    return range(n * h // GH, n * (h + 1) // GH)


def first_steps():
    def stats(c):
        return [("stats", 4 * c, 4 * c + 4), ("root", 4 * c, 4 * c + 4)]

    def chunk(kind, c, size=4):
        return [(kind, t) for t in range(size * c, size * (c + 1))]

    steps = stats(0) + stats(1) + chunk("norm", 0) + stats(2) + chunk("norm", 1) + chunk("nT", 0, 2)
    steps += [("split", 0), ("split", 1)] + stats(3) + chunk("norm", 2) + chunk("nT", 1, 2) + chunk("kv", 0)
    steps += chunk("norm", 3) + chunk("nT", 2, 2) + [("kn", 0)] + chunk("kv", 1) + [("kT", 0), ("v", 0)]
    steps += chunk("nT", 3, 2) + [("kn", 1)] + chunk("kv", 2) + [("kT", 1), ("v", 1)]
    steps += [("kn", 2), ("q", 0), ("q_square", 0)] + chunk("kv", 3) + [("kT", 2), ("kn", 3), ("v", 2), ("qT", 0), ("q_sums", 0)]
    return steps + [("q_scale", 0), ("kT", 3), ("v", 3)]


def next_head(j):
    if j < 0:
        return [("split", 0), ("split", 1)] + [("kv", t) for t in range(6)]
    steps = {0: [("kv", 6), ("kn", 0)], 1: [("kv", 7)], 2: [("kv", 8), ("kT", 0)], 3: [("kv", 9), ("kn", 1)],
             4: [("kv", 10)], 5: [("kv", 11), ("kT", 1)], 6: [("q", 0), ("kn", 2), ("q_square", 0), ("v", 0)],
             7: [("kv", 12)], 8: [("kv", 13), ("kT", 2)], 9: [("kv", 14), ("q_sums", 0), ("q_scale", 0)],
             10: [("kv", 15), ("v", 1)], 12: [("kn", 3)], 14: [("v", 2)]}
    return steps.get(j, [])


def second_layernorm(j):
    if j < 0:
        return [("norm", t) for t in range(4, 8)] + [("nT", r) for r in range(4)] + [("pads",)]
    steps = []
    if j in (1, 2, 3, 4):
        steps.append(("norm", 7 + j))
    if j == 3:
        steps += [("stats", NT - 4, NT - 1), ("root", NT - 4, NT - 1)]
    due = {0: ("ffw", 6), 2: ("ffw", 7), 3: ("ffw", 8), 5: ("nT", 4), 6: ("nT", 5), 8: ("ffw", 0), 10: ("ffw", 1), 12: ("ffw", 2)}
    return steps + ([due[j]] if j in due else [])


def group_steps(last):
    steps = [("q", 1), ("q_square", 1)]
    beside = second_layernorm if last else next_head
    products, projections = [], []

    def finish(unit):
        steps.extend(("wo", u) for u in projections)
        steps.extend(("pv",) + p for p in products)
        products.clear()
        steps.append(("outT", unit))
        projections[:] = [unit]

    for i in range(NT + 1):
        sums_head = 1 if i == 0 else 0
        for h in range(GH):
            scores = [("score", i, h, b) for b in range(len(score_blocks(i)))] if i < NT else []
            tiles = quarter(i, h)
            half = len(scores)
            if i == NT and h == 0:
                steps.append(("inv",))
                if last:
                    steps += [("norm", t) for t in range(4)]
            if i >= 2 and 0 in tiles:
                half = (half + 1) // 2
                steps += scores[:half]
                finish(i - 2)
                steps += scores[half:]
            else:
                steps += scores
            if i == NT and h == 0:
                steps += beside(-1)
            for j in tiles:
                steps.append(("pT", i - 1, j))
                if j >= 1 and projections:
                    steps.append(("wo", projections.pop()))
                products.append((i - 1, j))
                if len(products) > LAG:
                    steps.append(("pv",) + products.pop(0))
                if i == NT:
                    steps += beside(j)
            if h == 2 and i < NT - 2:
                steps.append(("q", i + 2))
            if h == sums_head and i < NT - 1:
                steps.append(("q_sums", i + 1))
            if h == 0 and i < NT - 1:
                steps.append(("qT", i + 1))
            if i < NT:
                steps.append(("end", i, h))
            if h == sums_head and i < NT - 1:
                steps.append(("q_scale", i + 1))
            if h == 2 and i < NT - 2:
                steps.append(("q_square", i + 2))
            if (i, h) == (0, 3):
                steps.append(("split", 2))
            if last and h == 3 and i < NT and i % 4 == 1 and i > 4:
                steps += [("stats", i - 5, i - 1), ("root", i - 5, i - 1)]
    finish(NT - 1)
    if last:
        steps += [("ffw", n) for n in (3, 4, 5)]
        steps += [("norm", NT - 4), ("norm", NT - 3), ("nT", 6), ("norm", NT - 2)]
        steps += [("wo", NT - 1), ("stats", NT - 1, NT), ("root", NT - 1, NT), ("norm", NT - 1)]
        return steps + [("gate_up", 0, 0), ("nT", 7)]
    return steps + [("kT", 3), ("qT", 0), ("v", 3), ("wo", NT - 1)]


def scalar_steps(steps):
    out, exps = [], []
    for step in steps:
        if step[0] == "score":
            exps.append(step)
        elif step[0] in ("q", "end"):
            out += exps + [step]
            exps = []
        else:
            out.append(step)
            if step[0] in ("pT", "qT") and exps:
                out.append(exps.pop(0))
    return out


def numbered(steps, kinds):
    found = [s for s in steps if s[0] in kinds]
    return {s: n for n, s in enumerate(found)}, len(found)


class Part:
    def __init__(self, steps, before, looped=False):
        self.steps = steps
        self.before = before
        self.slot, slots = numbered(steps, ("kv", "q", "score"))
        self.tslot, tslots = numbered(steps, ("nT", "kT", "qT", "pT", "wo", "ffw"))
        self.hslot, hslots = numbered(steps, ("nT", "kT", "qT", "pT", "ffw"))
        self.last_counts = 1 + -tslots % TBANKS if looped else 1
        self.sizes = (slots, tslots + self.last_counts - 1, hslots)
        self.looped = looped

        self.layernorm = 0 if before[0] == 0 else 1
        self.roots = [s for s in steps if s[0] == "root"]
        self.roots_before = 4 * self.layernorm

    def root_number(self, t):
        return self.roots_before + 1 + [a <= t < b for _, a, b in self.roots].index(True)

    def number(self, which, found, step, g):
        at = self.before[which] + found[step]
        return g * self.sizes[which] + at if self.looped else at

    def slot_number(self, step, g):
        return self.number(0, self.slot, step, g)

    def t_number(self, step, g):
        return self.number(1, self.tslot, step, g)

    def h_number(self, step, g):
        return self.number(2, self.hslot, step, g)

    def after(self, times=1):
        return tuple(b + times * n for b, n in zip(self.before, self.sizes))


def block_kernel(nc, x, Wq, Wk, Wv, Wo, gq, gk, gate_w, up_w, down_w, gate_s, up_s, down_s, out):
    first = Part(first_steps(), (0, 0, 0))
    middle = Part(group_steps(last=False), first.after(), looped=True)
    final = Part(group_steps(last=True), middle.after(GROUPS - 1))
    T_END = final.after()[1]
    pv, pvs = numbered(middle.steps, ("pv",))
    score_count = numbered(middle.steps, ("score",))[1]
    assert middle.sizes[0] % 4 == 0 and middle.sizes[1] % TBANKS == 0 and pvs % PBUFS == 0 and NT % 2 == 0
    long_rows = [i for i in range(NT) if len(score_blocks(i)) > 1]
    ctx = ExitStack()
    with ctx:
        def sb(name, shape, dt):
            return ctx.enter_context(nc.sbuf_tensor(name, shape, dt))

        def sem(name):
            return ctx.enter_context(nc.semaphore(name))

        x1 = sb("x1", [P, NT * HID], fp32)
        normT_hi = sb("normT_hi", [P, CT, ROWS], fp32r)
        normT_lo = sb("normT_lo", [P, CT, ROWS], fp32r)
        w_raw = sb("w_raw", [P, WCOLS], fp32)
        w_hi = sb("w_hi", [P, WCOLS], fp32r)
        w_lo = sb("w_lo", [P, WCOLS], fp32r)
        kT_hi = sb("kT_hi", [P, ROWS], fp32r)
        kT_lo = sb("kT_lo", [P, ROWS], fp32r)
        v_hi = sb("v_hi", [P, NT * D], fp32r)
        v_lo = sb("v_lo", [P, NT * D], fp32r)
        q_rows = sb("q_rows", [P, QW], fp32)
        q_sqr = sb("q_sqr", [P, QW], fp32)
        qT_hi = sb("qT_hi", [P, 2, QW], fp32r)
        qT_lo = sb("qT_lo", [P, 2, QW], fp32r)
        probs = [sb("probs_even", [P, GH, (NT - 1) * P], fp32), sb("probs_odd", [P, GH, NT * P], fp32)]
        pT_hi = sb("pT_hi", [P, PBUFS, QW], fp32r)
        pT_lo = sb("pT_lo", [P, PBUFS, QW], fp32r)
        outT_hi = sb("outT_hi", [P, QW], fp32r)
        outT_lo = sb("outT_lo", [P, QW], fp32r)
        ident = sb("ident", [P, P], fp32)
        ident_b = sb("ident_b", [P, P], bf16)
        mask_b = sb("mask_b", [P, P], bf16)
        half_neg = sb("half_neg", [P, NT], fp32)
        bn = sb("bn", [P, NT, 6], fp32)
        mean_var = sb("mean_var", [P, NT, 2], fp32)
        rstd = sb("rstd", [P, NT], fp32)
        gain_q = sb("gain_q", [P, 1], fp32)
        gain_k = sb("gain_k", [P, 1], fp32)
        gain = sb("gain", [P, 1], fp32)
        k_ssq = sb("k_ssq", [P, NT], fp32)
        k_var = sb("k_var", [P, NT], fp32)
        k_rstd = sb("k_rstd", [P, NT], fp32)
        q_ssq = sb("q_ssq", [P, 2, GH], fp32)
        q_var = sb("q_var", [P, 2, GH], fp32)
        q_scale = sb("q_scale", [P, 2, GH], fp32)
        q_scale_neg = sb("q_scale_neg", [P, 2, GH], fp32)
        block_max = sb("block_max", [P, 2, GH, 4], fp32)
        scaled_max = sb("scaled_max", [P, 2, GH, 4], fp32)
        bias = sb("bias", [P, 2, GH], fp32)
        block_sum = sb("block_sum", [P, 2, GH, 4], fp32)
        row_sum = sb("row_sum", [P, 2, GH], fp32)
        row_inv = sb("row_inv", [P, 2, GH], fp32)
        gate_half = sb("gate_half", [P, MT], fp32)
        gate_col = sb("gate_col", [P, MT], fp32)
        up_col = sb("up_col", [P, MT], fp32)
        down_row = sb("down_row", [P, HID], fp32)

        odd = probs[1][:, :, :].rearrange("p h n -> p (h n)")
        ff = odd[:, 0:8 * CHUNK].rearrange("p (k a n) -> p k a n", k=4, a=2)
        ff_tanh, ff_gate, ff_part, ff_hidden = (ff[:, k, :, :] for k in range(4))
        y_part = odd[:, 8 * CHUNK:8 * CHUNK + TPC * HID].rearrange("p (t n) -> p t n", n=HID)
        even = probs[0][:, :, :].rearrange("p h n -> p (h n)")
        rows = even[:, 0:NT * HID].rearrange("p (t c) -> p t c", c=HID)
        kv_rows = rows
        rest = even[:, NT * HID:]
        squares = rest[:, 0:NT * D].rearrange("p (t d) -> p t d", d=D)
        gate_raw = rest[:, 0:MT * HID].rearrange("p (m c) -> p m c", c=HID)
        up_raw = rest[:, MT * HID:2 * MT * HID].rearrange("p (m c) -> p m c", c=HID)
        down_raw = w_raw[:, 0:CT * IPAD].rearrange("p (r i) -> p r i", i=IPAD)
        ffw = [(kT_hi, kT_lo), (v_hi, v_lo), (w_hi, w_lo)]

        slot_bank = [ctx.enter_context(nc.psum_tensor(f"slot{n}", [P, BANK], fp32)) for n in range(4)]
        tslot_bank = [ctx.enter_context(nc.psum_tensor(f"tslot{n}", [P, BANK], fp32)) for n in range(TBANKS)]
        outT_bank = ctx.enter_context(nc.psum_tensor("outT", [P, BANK], fp32))
        down_bank = tslot_bank + [outT_bank]

        x_in = [sem(f"x_in{c}") for c in range(4)]
        gains_in = sem("gains_in")
        ff_scales_in = sem("ff_scales_in")
        ffw_in = sem("ffw_in")
        wkvq_in = sem("wkvq_in")
        wo_in = sem("wo_in")
        y_out = sem("y_out")
        consts = sem("consts")
        pool_waits = sem("pool_waits")
        ident_zero = sem("ident_zero")
        gains_ready = sem("gains_ready")
        pads_ready = sem("pads_ready")
        bn_done = sem("bn_done")
        aggr_done = sem("aggr_done")
        var_done = sem("var_done")
        rstd_ready = sem("rstd_ready")
        norm_ready = sem("norm_ready")
        w_hi_done = sem("w_hi_done")
        w_split = sem("w_split")
        slot_full = sem("slot_full")
        slot_free = sem("slot_free")
        t_full = sem("t_full")
        t_hi = sem("t_hi")
        t_free = sem("t_free")
        k_var_done = sem("k_var_done")
        k_rstd_ready = sem("k_rstd_ready")
        k_normed = sem("k_normed")
        v_hi_done = sem("v_hi_done")
        v_ready = sem("v_ready")
        q_sqr_done = sem("q_sqr_done")
        q_ssq_done = sem("q_ssq_done")
        q_var_done = sem("q_var_done")
        q_root_done = sem("q_root_done")
        q_scale_ready = sem("q_scale_ready")
        max_done = sem("max_done")
        bias_ready = sem("bias_ready")
        sum_done = sem("sum_done")
        inv_ready = sem("inv_ready")
        probs_ready = sem("probs_ready")
        pv_done = sem("pv_done")
        out_hi = sem("out_hi")
        out_ready = sem("out_ready")
        gate_full = sem("gate_full")
        up_full = sem("up_full")
        gate_read = sem("gate_read")
        up_read = sem("up_read")
        ff_part_done = sem("ff_part_done")
        ff_hi = sem("ff_hi")
        ff_ready = sem("ff_ready")
        down_step = sem("down_step")
        down_read = sem("down_read")
        y_scaled = sem("y_scaled")
        y_ready = sem("y_ready")

        block = ctx.enter_context(nc.Block())

        @block.sync
        def _(sp):
            xv = x[0].rearrange("(k t p) c -> k p t c", p=P, t=TPC)
            x1v = x1[:, :].rearrange("p (k t c) -> p k t c", k=4, c=HID)
            for c in range(4):
                sp.dma_start(x1v[:, c, :, :], xv[c]).then_inc(x_in[c], 16)

            def load_kvq(g):
                wkv = w_raw[:, WKV0:WO0].rearrange("p (c n) -> p c n", c=CT)
                sp.dma_start(wkv[:, :, 0:D], Wk.rearrange("(c p) n -> p c n", p=P)[:, :, bass.ds(g * D, D)]).then_inc(wkvq_in, 16)
                sp.dma_start(wkv[:, :, D:2 * D], Wv.rearrange("(c p) n -> p c n", p=P)[:, :, bass.ds(g * D, D)]).then_inc(wkvq_in, 16)
                sp.dma_start(w_raw[:, WQ0:WKV0].rearrange("p (c n) -> p c n", c=CT),
                             Wq.rearrange("(c p) n -> p c n", p=P)[:, :, bass.ds(g * QW, QW)]).then_inc(wkvq_in, 16)

            def load_o(g):
                sp.dma_start(w_raw[:, WO0:WCOLS].rearrange("p (h n) -> p h n", h=GH),
                             Wo.rearrange("(g h p) n -> g p h n", h=GH, p=P)[bass.ds(g, 1), :, :, :].rearrange("g p h n -> (g p) h n")).then_inc(wo_in, 16)

            load_kvq(0)
            load_o(0)
            with sp.Fori(0, GROUPS - 1) as g:
                sp.wait_ge(w_split, 3 * g + 3)
                load_kvq(g + 1)
                sp.wait_ge(w_split, 3 * g + 4)
                load_o(g + 1)
            sp.wait_ge(w_split, 3 * GROUPS + 1)
            sp.dma_start(down_raw[:, :, 0:INTER], down_w.rearrange("(r p) i -> p r i", p=P)).then_inc(ffw_in, 16)
            sp.wait_ge(t_full, final.t_number(("pT", NT - 2, NT - 2), None) + 1)
            full = MT - 1
            for src, dst in ((gate_w, gate_raw), (up_w, up_raw)):
                sp.dma_start(dst[:, 0:full, :], src[0:full * P, :].rearrange("(m p) c -> p m c", p=P)).then_inc(ffw_in, 16)
                sp.dma_start(dst[0:INTER - full * P, full, :], src[full * P:INTER, :]).then_inc(ffw_in, 16)
            with sp.Fori(0, NCH) as k:
                outv = out[0].rearrange("(k t p) c -> k p t c", p=P, t=TPC)
                for t in range(TPC):
                    sp.wait_ge(y_ready, k * TPC + t + 1)
                    sp.dma_start(outv[bass.ds(k, 1), :, t, :].rearrange("k p c -> (k p) c"),
                                 x1[:, bass.ds(k * (TPC * HID) + t * HID, HID)]).then_inc(y_out, 16)
            sp.wait_ge(y_out, 16 * NT)

        @block.gpsimd
        def _(pool):
            nc.gpsimd.memset(half_neg[:, :], -0.5).then_inc(consts, 1)
            nc.gpsimd.memset(ident[:, :], 0.0).then_inc(ident_zero, 1)
            nc.gpsimd.memset(mask_b[:, :], 0.0).then_inc(ident_zero, 1)
            pool.wait_ge(ident_zero, 2)
            nc.gpsimd.affine_select(out=ident[:, :], in_=ident[:, :], compare_op=ALU.not_equal, fill=1.0,
                                    base=0, pattern=[[-1, P]], channel_multiplier=1).then_inc(consts, 1)
            nc.gpsimd.affine_select(out=mask_b[:, :], in_=mask_b[:, :], compare_op=ALU.is_ge, fill=MASKED,
                                    base=0, pattern=[[-1, P]], channel_multiplier=1).then_inc(consts, 1)
            pool.wait_ge(consts, 3)
            nc.gpsimd.tensor_copy(ident_b[:, :], ident[:, :]).then_inc(consts, 1)

            def layernorm_root(part, step):
                n = part.layernorm
                t = slice(step[1], step[2])
                pool.wait_ge(aggr_done, n * NT + step[2])
                nc.gpsimd.tensor_scalar(rstd[:, t], mean_var[:, t, 1], 1.0, LN_EPS,
                                        ALU.mult, ALU.add).then_inc(var_done, 1)
                pool.wait_ge(var_done, part.root_number(step[1]))
                nc.gpsimd.tensor_tensor(rstd[:, t], rstd[:, t], half_neg[:, t], ALU.pow).then_inc(rstd_ready, 1)

            def wait_for(semaphore, value):
                pool.wait_ge(semaphore, value)
                pool.sem_inc(pool_waits, 1)

            def query_square(part, g, i):
                wait_for(slot_free, 4 + part.slot_number(("q", i), g) + 1)
                nc.gpsimd.tensor_tensor(q_sqr[:, :], q_rows[:, :], q_rows[:, :], ALU.mult).then_inc(q_sqr_done, 1)

            def query_scale(g, i):
                a = i % 2
                wait_for(q_ssq_done, g * NT + i + 1)
                nc.gpsimd.tensor_scalar(q_var[:, a, :], q_ssq[:, a, :], 1.0, D * RMS_EPS,
                                        ALU.mult, ALU.add).then_inc(q_var_done, 1)
                wait_for(q_var_done, g * NT + i + 1)
                nc.gpsimd.tensor_tensor(q_scale[:, a, :], q_var[:, a, :], half_neg[:, 0:GH], ALU.pow).then_inc(q_root_done, 1)
                wait_for(q_root_done, g * NT + i + 1)
                nc.gpsimd.tensor_scalar(q_scale_neg[:, a, :], q_scale[:, a, :], -1.0, 1.0,
                                        ALU.mult, ALU.mult).then_inc(q_scale_ready, 1)

            def run(part, g):
                for step in part.steps:
                    if step[0] == "root":
                        layernorm_root(part, step)
                    elif step[0] == "kn":
                        c = step[1]
                        t = slice(4 * c, 4 * c + 4)
                        wait_for(slot_free, 4 + part.slot_number(("kv", 4 * c + 3), g) + 1)
                        nc.gpsimd.tensor_scalar(k_var[:, t], k_ssq[:, t], 1.0 / D, RMS_EPS,
                                                ALU.mult, ALU.add).then_inc(k_var_done, 1)
                        wait_for(k_var_done, (g + 1) * 4 + c + 1)
                        nc.gpsimd.tensor_tensor(k_rstd[:, t], k_var[:, t], half_neg[:, t], ALU.pow).then_inc(k_rstd_ready, 1)
                    elif step[0] == "q_square":
                        query_square(part, g, step[1])
                    elif step[0] == "q_scale":
                        query_scale(g if step[1] else g + 1, step[1])
                    elif step[0] == "end":
                        _, i, h = step
                        wait_for(inv_ready, g * NT * GH + i * GH + h + 1)
                        row = probs[i % 2][:, h, 0:(i + 1) * P]
                        nc.gpsimd.tensor_scalar(row, row, row_inv[:, i % 2, h:h + 1], 1.0,
                                                ALU.mult, ALU.mult).then_inc(probs_ready, 1)

            run(first, -1)
            with pool.Fori(0, GROUPS - 1) as g:
                run(middle, g)
            run(final, GROUPS - 1)

        @block.scalar
        def _(act):
            act.sem_inc(slot_free, 4)
            act.sem_inc(gate_read, 2)
            for dst, src in ((gain_q, gq), (gain_k, gk)):
                act.dma_start(dst[:, :], src.rearrange("(p a) -> p a", a=1)).then_inc(gains_in, 16)
            full = MT - 1
            act.wait_ge(pads_ready, 2)
            for dst, src in ((gate_col, gate_s), (up_col, up_s)):
                act.dma_start(dst[:, 0:full], src[0:full * P].rearrange("(m p) -> p m", p=P),
                              allow_slow_non_contiguous=True).then_inc(ff_scales_in, 16)
                act.dma_start(dst[0:INTER - full * P, full:MT],
                              src[full * P:INTER].rearrange("(p a) -> p a", a=1)).then_inc(ff_scales_in, 16)
            act.dma_start(down_row[:, :], down_s.partition_broadcast(P)).then_inc(ff_scales_in, 16)

            def run(part, g):
                for step in scalar_steps(part.steps):
                    if step in part.slot:
                        bank = slot_bank[part.slot_number(step, 0) % 4]
                        slot_filled = part.slot_number(step, g) + 1
                    elif step in part.tslot:
                        bank = tslot_bank[part.t_number(step, 0) % TBANKS]
                        tslot_filled = part.t_number(step, g) + 1
                    if step[0] == "split":
                        n = step[1]
                        if n < 2:
                            act.wait_ge(wkvq_in, 48 * (g + 1) + 48)
                        else:
                            act.wait_ge(wo_in, 16 * g + 16)
                        a, b = W_PARTS[n]
                        nc.scalar.activation(w_hi[:, a:b], w_raw[:, a:b], ACT.Copy).then_inc(w_hi_done, 1)
                    elif step[0] == "nT":
                        r = step[1]
                        act.wait_ge(t_full, tslot_filled)
                        nc.scalar.activation(normT_hi[:, :, 2 * r * P:2 * (r + 1) * P],
                                             bank[:, :].rearrange("p (c n) -> p c n", c=CT), ACT.Copy).then_inc(t_hi, 1)
                    elif step[0] == "kv":
                        t = step[1]
                        act.wait_ge(slot_full, slot_filled)
                        nc.scalar.activation(squares[:, t, :], bank[:, 0:D], ACT.Square, accum_out=k_ssq[:, t:t + 1])
                        nc.scalar.activation(kv_rows[:, t, :], bank[:, 0:2 * D], ACT.Copy).then_inc(slot_free, 1)
                    elif step[0] == "kT":
                        c = step[1]
                        act.wait_ge(t_full, tslot_filled)
                        nc.scalar.activation(kT_hi[:, c * BANK:(c + 1) * BANK], bank[:, :],
                                             ACT.Copy, scale=gain[:, 0:1]).then_inc(t_hi, 1)
                    elif step[0] == "v":
                        c = step[1]
                        if part is not first:
                            act.wait_ge(pv_done, PBUFS + g * pvs + pv[("pv", NT - 1, 4 * c + 3)] + 1)
                        act.wait_ge(slot_free, 4 + part.slot_number(("kv", 4 * c + 3), g) + 1)
                        nc.scalar.activation(v_hi[:, 4 * c * D:(4 * c + 4) * D].rearrange("p (t d) -> p t d", d=D),
                                             kv_rows[:, 4 * c:4 * c + 4, D:2 * D], ACT.Copy).then_inc(v_hi_done, 1)
                    elif step[0] == "q":
                        i = step[1]
                        if i or part is not first:
                            act.wait_ge(q_ssq_done, g * NT + (i or NT))
                        act.wait_ge(slot_full, slot_filled)
                        nc.scalar.activation(q_rows[:, :], bank[:, :], ACT.Copy).then_inc(slot_free, 1)
                    elif step[0] == "qT":
                        act.wait_ge(t_full, tslot_filled)
                        nc.scalar.activation(qT_hi[:, step[1] % 2, :], bank[:, :], ACT.Copy).then_inc(t_hi, 1)
                    elif step[0] == "score":
                        _, i, h, b = step
                        start, width = score_blocks(i)[b]
                        if b == 0:
                            act.wait_ge(bias_ready, g * NT * GH + i * GH + h + 1)
                        nc.scalar.activation(probs[i % 2][:, h, start:start + width], bank[:, 0:width], ACT.Exp,
                                             bias=bias[:, i % 2, h:h + 1], scale=q_scale[:, i % 2, h:h + 1],
                                             accum_out=block_sum[:, i % 2, h, b:b + 1]).then_inc(slot_free, 1)
                    elif step[0] == "pT":
                        n = pv[("pv",) + step[1:]]
                        act.wait_ge(t_full, tslot_filled)
                        act.wait_ge(pv_done, g * pvs + n + 1)
                        nc.scalar.activation(pT_hi[:, n % PBUFS, :], bank[:, :], ACT.Copy).then_inc(t_hi, 1)
                    elif step[0] == "outT":
                        i = step[1]
                        act.wait_ge(pv_done, PBUFS + g * pvs + pv[("pv", i, i)] + 1)
                        nc.scalar.activation(outT_hi[:, :], outT_bank[:, :], ACT.Copy).then_inc(out_hi, 1)
                    elif step[0] == "ffw":
                        n = step[1]
                        hi, m = ffw[n // (MT // 2)][0], n % (MT // 2)
                        act.wait_ge(t_full, tslot_filled)
                        src = bank[:, :]
                        if n // (MT // 2) < 2:
                            dst = hi[:, 0:CT * IPAD].rearrange("p (c i) -> p c i", c=CT)[:, :, 2 * m * P:2 * (m + 1) * P]
                            src = src.rearrange("p (c n) -> p c n", c=CT)
                        else:
                            dst = hi[:, m * BANK:(m + 1) * BANK]
                        nc.scalar.activation(dst, src, ACT.Copy).then_inc(t_hi, 1)

            run(first, -1)
            with act.Fori(0, GROUPS - 1) as g:
                run(middle, g)
            run(final, GROUPS - 1)

            with act.Fori(0, NCH) as k:
                for m in range(MT):
                    a = m % 2
                    g_bank = slot_bank[2 * a]
                    act.wait_ge(gate_full, k * MT + m + 1)
                    nc.scalar.activation(ff_tanh[:, a, :], g_bank[:, :], ACT.Tanh, scale=gate_half[:, m:m + 1])
                    nc.scalar.activation(ff_gate[:, a, :], g_bank[:, :], ACT.Copy,
                                         scale=gate_half[:, m:m + 1]).then_inc(gate_read, 1)
                    act.wait_ge(up_read, 2 + k * MT + m + 1)
                    act.wait_ge(down_step, k * MT + m + 1)
                    nc.scalar.activation(pT_hi[:, a, :], ff_hidden[:, a, :], ACT.Copy).then_inc(ff_hi, 1)

        @block.vector
        def _(dve):
            dve.sem_inc(w_split, 1)
            dve.sem_inc(t_free, TBANKS)
            dve.sem_inc(out_ready, 1)
            dve.sem_inc(up_read, 2)
            dve.sem_inc(down_read, 4)
            nc.vector.memset(gate_col[:, :], 0.0).then_inc(pads_ready, 1)
            nc.vector.memset(up_col[:, :], 0.0).then_inc(pads_ready, 1)

            dve.wait_ge(gains_in, 16 * 2)
            nc.vector.tensor_tensor(gain[:, :], gain_q[:, :], gain_k[:, :], ALU.mult).then_inc(gains_ready, 1)

            def query_sums(g, i):
                dve.wait_ge(q_sqr_done, g * NT + i + 1)
                nc.vector.reduce_sum(q_ssq[:, i % 2, :], q_sqr[:, :].rearrange("p (h d) -> p h d", d=D),
                                     AX.X).then_inc(q_ssq_done, 1)

            def row_inverse(part, g, i, h):
                a, nb = i % 2, len(score_blocks(i))
                dve.wait_ge(slot_free, 4 + part.slot_number(("score", i, h, nb - 1), g) + 1)
                total = block_sum[:, a, h, 0:1]
                if nb > 1:
                    nc.vector.reduce_sum(row_sum[:, a, h:h + 1], block_sum[:, a, h, 0:nb], AX.X).then_inc(sum_done, 1)
                    dve.wait_ge(sum_done, g * GH * len(long_rows) + GH * long_rows.index(i) + h + 1)
                    total = row_sum[:, a, h:h + 1]
                nc.vector.reciprocal(row_inv[:, a, h:h + 1], total).then_inc(inv_ready, 1)

            def run(part, g):
                rows_due = []
                for step in part.steps:
                    if step in part.slot:
                        bank = slot_bank[part.slot_number(step, 0) % 4]
                    elif step in part.tslot:
                        bank = tslot_bank[part.t_number(step, 0) % TBANKS]
                        if step[0] != "wo":
                            dve.wait_ge(t_hi, part.h_number(step, g) + 1)
                    if step[0] == "split":
                        n = step[1]
                        a, b = W_PARTS[n]
                        dve.wait_ge(w_hi_done, 3 * g + (n + 1 if n == 2 else n + 4))
                        nc.vector.tensor_tensor(w_lo[:, a:b], w_raw[:, a:b], w_hi[:, a:b].bitcast(fp32),
                                                ALU.subtract).then_inc(w_split, 1)
                    elif step[0] == "stats":
                        tiles = range(step[1], step[2])
                        if part is first:
                            dve.wait_ge(x_in[step[1] // 4], 16)
                        else:
                            dve.wait_ge(t_free, TBANKS + part.t_number(("wo", tiles[-1]), g) + 1)
                        for t in tiles:
                            nc.vector.bn_stats(bn[:, t, :], x1[:, t * HID:(t + 1) * HID]).then_inc(bn_done, 1)
                        for t in tiles:
                            dve.wait_ge(bn_done, part.layernorm * NT + t + 1)
                            nc.vector.bn_aggr(mean_var[:, t, :], bn[:, t, :]).then_inc(aggr_done, 1)
                    elif step[0] == "norm":
                        t = step[1]
                        dve.wait_ge(rstd_ready, part.root_number(t))
                        nc.vector.tensor_scalar(rows[:, t, :], x1[:, t * HID:(t + 1) * HID], mean_var[:, t, 0:1],
                                                rstd[:, t:t + 1], ALU.subtract, ALU.mult).then_inc(norm_ready, 1)
                    elif step[0] == "nT":
                        cols = slice(2 * step[1] * P, 2 * (step[1] + 1) * P)
                        nc.vector.tensor_tensor(normT_lo[:, :, cols], bank[:, :].rearrange("p (c n) -> p c n", c=CT),
                                                normT_hi[:, :, cols].bitcast(fp32), ALU.subtract).then_inc(t_free, 1)
                    elif step[0] == "kn":
                        c = step[1]
                        dve.wait_ge(k_rstd_ready, 4 * g + 4 + c + 1)
                        for t in range(4 * c, 4 * c + 4):
                            nc.vector.tensor_scalar(kv_rows[:, t, 0:D], kv_rows[:, t, 0:D], k_rstd[:, t:t + 1], None,
                                                    ALU.mult).then_inc(k_normed, 1)
                    elif step[0] == "v":
                        c = step[1]
                        dve.wait_ge(v_hi_done, 4 * g + 4 + c + 1)
                        cols = slice(4 * c * D, (4 * c + 4) * D)
                        nc.vector.tensor_tensor(v_lo[:, cols].rearrange("p (t d) -> p t d", d=D),
                                                kv_rows[:, 4 * c:4 * c + 4, D:2 * D],
                                                v_hi[:, cols].bitcast(fp32).rearrange("p (t d) -> p t d", d=D),
                                                ALU.subtract).then_inc(v_ready, 1)
                    elif step[0] == "kT":
                        c = step[1]
                        nc.vector.scalar_tensor_tensor(out=kT_lo[:, c * BANK:(c + 1) * BANK],
                                                       in0=bank[:, :], scalar=gain[:, 0:1],
                                                       in1=kT_hi[:, c * BANK:(c + 1) * BANK].bitcast(fp32),
                                                       op0=ALU.mult, op1=ALU.subtract).then_inc(t_free, 1)
                    elif step[0] == "qT":
                        a = step[1] % 2
                        nc.vector.tensor_tensor(qT_lo[:, a, :], bank[:, :],
                                                qT_hi[:, a, :].bitcast(fp32), ALU.subtract).then_inc(t_free, 1)
                    elif step[0] == "score":
                        _, i, h, b = step
                        a, blocks = i % 2, score_blocks(i)
                        dve.wait_ge(slot_full, part.slot_number(step, g) + 1)
                        nc.vector.tensor_reduce(block_max[:, a, h, b:b + 1], bank[:, 0:blocks[b][1]],
                                                AX.X, ALU.max).then_inc(max_done, 1)
                        if b == 0 and rows_due:
                            row_inverse(part, g, *rows_due.pop())
                        if b == len(blocks) - 1:
                            if h == 0:
                                dve.wait_ge(q_scale_ready, g * NT + i + 1)
                            done = sum(GH * len(score_blocks(u)) for u in range(i)) + (h + 1) * len(blocks)
                            dve.wait_ge(max_done, g * score_count + done)
                            nc.vector.tensor_scalar(scaled_max[:, a, h, 0:len(blocks)], block_max[:, a, h, 0:len(blocks)],
                                                    q_scale_neg[:, a, h:h + 1], None, ALU.mult, ALU.min,
                                                    accum_out=bias[:, a, h:h + 1]).then_inc(bias_ready, 1)
                            rows_due.append((i, h))
                    elif step[0] == "inv":
                        row_inverse(part, g, *rows_due.pop())
                    elif step[0] == "pT":
                        n = pv[("pv",) + step[1:]]
                        nc.vector.tensor_tensor(pT_lo[:, n % PBUFS, :], bank[:, :],
                                                pT_hi[:, n % PBUFS, :].bitcast(fp32), ALU.subtract).then_inc(t_free, 1)
                    elif step[0] == "outT":
                        i = step[1]
                        dve.wait_ge(out_hi, g * NT + i + 1)
                        nc.vector.tensor_tensor(outT_lo[:, :], outT_bank[:, :], outT_hi[:, :].bitcast(fp32),
                                                ALU.subtract).then_inc(out_ready, 1)
                    elif step[0] == "wo":
                        i = step[1]
                        dve.wait_ge(t_full, part.t_number(step, g) + 1)
                        cols = slice(i * HID, (i + 1) * HID)
                        nc.vector.tensor_tensor(x1[:, cols], bank[:, 0:HID], x1[:, cols],
                                                ALU.add).then_inc(t_free, part.last_counts if i == NT - 1 else 1)
                    elif step[0] == "q_sums":
                        query_sums(g + 1 if step[1] == 0 else g, step[1])
                    elif step[0] == "pads":
                        full = MT - 1
                        nc.vector.memset(gate_raw[64:P, full, :], 0.0).then_inc(pads_ready, 1)
                        nc.vector.memset(up_raw[64:P, full, :], 0.0).then_inc(pads_ready, 1)
                        nc.vector.memset(down_raw[:, :, INTER:IPAD], 0.0).then_inc(pads_ready, 1)
                    elif step[0] == "ffw":
                        n = step[1]
                        (hi, lo), m = ffw[n // (MT // 2)], n % (MT // 2)
                        src = bank[:, :]
                        if n // (MT // 2) < 2:
                            cols = slice(2 * m * P, 2 * (m + 1) * P)
                            hi = hi[:, 0:CT * IPAD].bitcast(fp32).rearrange("p (c i) -> p c i", c=CT)[:, :, cols]
                            lo = lo[:, 0:CT * IPAD].rearrange("p (c i) -> p c i", c=CT)[:, :, cols]
                            src = src.rearrange("p (c n) -> p c n", c=CT)
                        else:
                            hi, lo = hi[:, m * BANK:(m + 1) * BANK].bitcast(fp32), lo[:, m * BANK:(m + 1) * BANK]
                        nc.vector.tensor_tensor(lo, src, hi, ALU.subtract).then_inc(t_free, 1)

            run(first, -1)
            dve.wait_ge(ff_scales_in, 16 * 5)
            nc.vector.tensor_scalar(gate_half[:, :], gate_col[:, :], 0.5, None, ALU.mult).then_inc(gains_ready, 1)
            with dve.Fori(0, GROUPS - 1) as g:
                run(middle, g)
            run(final, GROUPS - 1)


            def hidden(k, m):
                a = m % 2
                dve.wait_ge(gate_read, 2 + k * MT + m + 1)
                nc.vector.scalar_tensor_tensor(out=ff_part[:, a, :], in0=ff_tanh[:, a, :], scalar=1.0,
                                               in1=ff_gate[:, a, :], op0=ALU.add, op1=ALU.mult).then_inc(ff_part_done, 1)
                dve.wait_ge(ff_part_done, k * MT + m + 1)
                dve.wait_ge(up_full, k * MT + m + 1)
                nc.vector.scalar_tensor_tensor(out=ff_hidden[:, a, :], in0=slot_bank[2 * a + 1][:, :],
                                               scalar=up_col[:, m:m + 1], in1=ff_part[:, a, :],
                                               op0=ALU.mult, op1=ALU.mult).then_inc(up_read, 1)
                dve.wait_ge(ff_hi, k * MT + m + 1)
                nc.vector.tensor_tensor(pT_lo[:, a, :], ff_hidden[:, a, :], pT_hi[:, a, :].bitcast(fp32),
                                        ALU.subtract).then_inc(ff_ready, 1)

            def output(k):
                dve.wait_ge(down_step, 2 + k * MT + MT)
                for t in range(TPC):
                    nc.vector.tensor_tensor(y_part[:, t, :], down_bank[t][:, 0:HID], down_row[:, :],
                                            ALU.mult).then_inc(down_read, 1)
                for t in range(TPC):
                    cols = bass.ds(k * (TPC * HID) + t * HID, HID)
                    dve.wait_ge(down_read, 4 + k * TPC + t + 1)
                    nc.vector.tensor_tensor(x1[:, cols], y_part[:, t, :], x1[:, cols], ALU.add).then_inc(y_ready, 1)

            hidden(0, 0)
            with dve.Fori(0, NCH - 1) as k:
                for m in range(1, MT):
                    hidden(k, m)
                hidden(k + 1, 0)
                output(k)
            for m in range(1, MT):
                hidden(NCH - 1, m)
            output(NCH - 1)

        @block.tensor
        def _(pe):
            pe.sem_inc(pv_done, PBUFS)
            pe.sem_inc(down_step, 2)

            def product3(bank, hi_l, lo_l, hi_r, lo_r, start, stop, masked=None):
                for n, (l, r) in enumerate(((hi_l, hi_r), (lo_l, hi_r), (hi_l, lo_r))):
                    last = nc.tensor.matmul(bank, l, r, start=start and n == 0, stop=stop and n == 2)
                    if n == 0 and masked is not None:
                        nc.tensor.matmul(masked, ident_b[:, :], mask_b[:, :], start=False, stop=False)
                return last

            def gate_up(k, m):
                a = m % 2
                for bank, (hi, lo), read, full in ((slot_bank[2 * a], ffw[0], gate_read, gate_full),
                                                   (slot_bank[2 * a + 1], ffw[1], up_read, up_full)):
                    pe.wait_ge(read, k * MT + m + 1)
                    for c in range(CT):
                        w = slice(c * IPAD + m * P, c * IPAD + (m + 1) * P)
                        cols = bass.ds(k * CHUNK, CHUNK)
                        last = product3(bank[:, :], hi[:, w], lo[:, w], normT_hi[:, c, cols], normT_lo[:, c, cols],
                                        start=(c == 0), stop=(c == CT - 1))
                    last.then_inc(full, 1)

            def run(part, g):
                for step in part.steps:
                    if step in part.slot:
                        bank = slot_bank[part.slot_number(step, 0) % 4]
                        slot_waits = part.slot_number(step, g) + 1
                    elif step in part.tslot:
                        bank = tslot_bank[part.t_number(step, 0) % TBANKS]
                        tslot_waits = part.t_number(step, g) + 1
                    if step[0] in ("kv", "q"):
                        t = step[1]
                        if step[0] == "kv" and part is first:
                            pe.wait_ge(t_free, TBANKS + part.t_number(("nT", t // 2), g) + 1)
                        if t == 0:
                            pe.wait_ge(w_split, 3 * g + (5 if step[0] == "kv" else 6))
                        pe.wait_ge(slot_free, slot_waits)
                        at, width = (WKV0, 2 * D) if step[0] == "kv" else (WQ0, QW)
                        for c in range(CT):
                            w = slice(at + c * width, at + (c + 1) * width)
                            last = product3(bank[:, 0:width],
                                            normT_hi[:, c, t * P:(t + 1) * P], normT_lo[:, c, t * P:(t + 1) * P],
                                            w_hi[:, w], w_lo[:, w], start=(c == 0), stop=(c == CT - 1))
                        last.then_inc(slot_full, 1)
                    elif step[0] == "nT":
                        r = step[1]
                        pe.wait_ge(norm_ready, part.layernorm * NT + 2 * r + 2)
                        pe.wait_ge(t_free, tslot_waits)
                        for c in range(CT):
                            for t in range(2):
                                at = (2 * c + t) * P
                                last = nc.tensor.transpose(bank[:, at:at + P], rows[:, 2 * r + t, c * P:(c + 1) * P], ident[:, :])
                        last.then_inc(t_full, 1)
                    elif step[0] in ("kT", "qT", "pT"):
                        if step[0] == "kT":
                            pe.wait_ge(k_normed, g * NT + NT + 4 * step[1] + 4)
                            tiles = [kv_rows[:, 4 * step[1] + t, 0:D] for t in range(4)]
                        elif step[0] == "qT":
                            pe.wait_ge(slot_free, 4 + part.slot_number(("q", step[1]), g) + 1)
                            tiles = [q_rows[:, h * D:(h + 1) * D] for h in range(GH)]
                        else:
                            _, i, j = step
                            if j == 0:
                                pe.wait_ge(probs_ready, g * NT * GH + (i + 1) * GH)
                            tiles = [probs[i % 2][:, h, j * P:(j + 1) * P] for h in range(GH)]
                        pe.wait_ge(t_free, tslot_waits)
                        for n, tile in enumerate(tiles):
                            last = nc.tensor.transpose(bank[:, n * P:(n + 1) * P], tile, ident[:, :])
                        last.then_inc(t_full, 1)
                    elif step[0] == "score":
                        _, i, h, b = step
                        start, width = score_blocks(i)[b]
                        diagonal = start + width == (i + 1) * P
                        if h == 0 and b == 0:
                            if i:
                                pe.wait_ge(t_free, TBANKS + part.t_number(("qT", i), g) + 1)
                            else:
                                pe.wait_ge(v_ready, 4 * g + 4)
                        q = slice(h * D, (h + 1) * D)
                        cols = slice(start, start + max(width, 2 * P))
                        pe.wait_ge(slot_free, slot_waits)
                        product3(bank[:, 0:max(width, 2 * P)], qT_hi[:, i % 2, q], qT_lo[:, i % 2, q],
                                 kT_hi[:, cols], kT_lo[:, cols], start=True, stop=True,
                                 masked=bank[:, width - P:width] if diagonal else None).then_inc(slot_full, 1)
                    elif step[0] == "pv":
                        _, i, j = step
                        n = pv[step]
                        if j == 0:
                            pe.wait_ge(out_ready, g * NT + i + 1)
                        pe.wait_ge(t_free, TBANKS + part.t_number(("pT", i, j), g) + 1)
                        product3(outT_bank[:, :], v_hi[:, j * D:(j + 1) * D], v_lo[:, j * D:(j + 1) * D],
                                 pT_hi[:, n % PBUFS, :], pT_lo[:, n % PBUFS, :], start=(j == 0), stop=(j == i)).then_inc(pv_done, 1)
                    elif step[0] == "wo":
                        i = step[1]
                        if i == 0:
                            pe.wait_ge(w_split, 3 * g + 4)
                        pe.wait_ge(out_ready, 1 + g * NT + i + 1)
                        pe.wait_ge(t_free, tslot_waits)
                        for h in range(GH):
                            o = slice(h * D, (h + 1) * D)
                            w = slice(WO0 + h * HID, WO0 + (h + 1) * HID)
                            last = product3(bank[:, 0:HID], outT_hi[:, o], outT_lo[:, o],
                                            w_hi[:, w], w_lo[:, w], start=(h == 0), stop=(h == GH - 1))
                        last.then_inc(t_full, part.last_counts if i == NT - 1 else 1)
                    elif step[0] == "gate_up":
                        pe.wait_ge(t_free, TBANKS + part.t_number(("ffw", 5), g) + 1)
                        gate_up(step[1], step[2])
                    elif step[0] == "ffw":
                        n = step[1]
                        m = n % (MT // 2)
                        pe.wait_ge(ffw_in, 16 * 5)
                        pe.wait_ge(pads_ready, 5)
                        pe.wait_ge(t_free, tslot_waits)
                        for a in range(2):
                            for b in range(2):
                                if n // (MT // 2) < 2:
                                    tile = (gate_raw, up_raw)[n // (MT // 2)][:, 2 * m + b, a * P:(a + 1) * P]
                                else:
                                    tile = down_raw[:, b, (2 * m + a) * P:(2 * m + a + 1) * P]
                                at = (2 * a + b) * P
                                last = nc.tensor.transpose(bank[:, at:at + P], tile, ident[:, :])
                        last.then_inc(t_full, 1)

            pe.wait_ge(consts, 4)
            run(first, -1)
            with pe.Fori(0, GROUPS - 1) as g:
                run(middle, g)
            run(final, GROUPS - 1)
            pe.wait_ge(t_free, TBANKS + T_END)

            def down(k, m):
                a = m % 2
                hi, lo = ffw[2]
                w = slice(m * HID, (m + 1) * HID)
                pe.wait_ge(ff_ready, k * MT + m + 1)
                for t in range(TPC):
                    if m == 0:
                        pe.wait_ge(down_read, k * TPC + t + 1)
                    r = slice(t * P, (t + 1) * P)
                    last = product3(down_bank[t][:, 0:HID], pT_hi[:, a, r], pT_lo[:, a, r], hi[:, w], lo[:, w],
                                    start=(m == 0), stop=(m == MT - 1))
                last.then_inc(down_step, 1)

            with pe.Fori(0, NCH - 1) as k:
                for m in range(MT):
                    if m < MT - 1:
                        gate_up(k, m + 1)
                    else:
                        gate_up(k + 1, 0)
                    down(k, m)
            for m in range(MT):
                if m < MT - 1:
                    gate_up(NCH - 1, m + 1)
                down(NCH - 1, m)


_INS = ["L0_attn_x", "L0_attn_Wq", "L0_attn_Wk", "L0_attn_Wv", "L0_attn_Wo", "L0_attn_gq", "L0_attn_gk",
        "L0_ffn_gate_w", "L0_ffn_up_w", "L0_ffn_down_w", "L0_ffn_gate_s", "L0_ffn_up_s", "L0_ffn_down_s"]
_OUT = ((1, ROWS, HID), "float32")


def kernel(**inputs):
    import numpy as _np
    import concourse.bacc as _bacc
    from concourse import mybir as _mybir
    from concourse.bass_utils import run_bass_kernel_spmd as _run

    nc = _bacc.Bacc("TRN2", target_bir_lowering=False, num_devices=1)
    arrays, args = {}, []
    for name in _INS:
        a = _np.ascontiguousarray(inputs[name])
        arrays[f"in_{name}_dram"] = a
        args.append(nc.dram_tensor(f"in_{name}_dram", a.shape, _mybir.dt.from_np(a.dtype), kind="ExternalInput").ap())
    args.append(nc.dram_tensor("out_dram", _OUT[0], _mybir.dt.from_np(_np.dtype(_OUT[1])), kind="ExternalOutput").ap())
    block_kernel(nc, *args)
    r = _run(nc, [arrays], core_ids=[0])
    return r.results[0]["out_dram"]
```
